# Optimizing a Trainium2 kernel written in Bass

```python
import numpy as np
import jax
import jax.numpy as jnp

def _softmax(x, axis=-1):
    return jax.nn.softmax(x, axis=axis)

def _gelu(x):
    return jax.nn.gelu(x, approximate=True)

def _silu(x):
    return jax.nn.silu(x)

def _sigmoid(x):
    return jax.nn.sigmoid(x)

def _layernorm(x, axis=-1, eps=1e-05):
    m = jnp.mean(x, axis=axis, keepdims=True)
    v = jnp.var(x, axis=axis, keepdims=True)
    return (x - m) / jnp.sqrt(v + eps)

def _scatter_add(tgt, idx, src, axis=0):
    return tgt.at[idx].add(src)

def _segment_sum(src, seg, n):
    return jax.ops.segment_sum(src, seg, n)
kernel_name = 'mk_decoder_postln_d1_seqx_r4_31ab53'

def setup_inputs(seed: int=0):
    np.random.seed(seed)
    _w = jnp.asarray

    def _rec_inputs():
        import jax
        import jax.numpy as jnp
        _rk = jax.random.key(seed)
        x = 7.22e-05 + 1 * jax.random.normal(jax.random.fold_in(_rk, 1), (4, 512, 512), jnp.float32)
        _lenS = 512 - jax.random.randint(jax.random.fold_in(_rk, 7), (4,), 0, max(1, 512 // 4) + 1, jnp.int32)
        _lenS2 = 512 - jax.random.randint(jax.random.fold_in(_rk, 8), (4,), 0, max(1, 512 // 4) + 1, jnp.int32)
        _ctx_2048P = jax.random.normal(jax.random.fold_in(_rk, 11), (4, 16, 512), jnp.float32)
        _ctx_2048c = jax.random.dirichlet(jax.random.fold_in(_rk, 511), 0.3 * jnp.ones((16,), jnp.float32), (4, 512))
        _ctx_2048t = jnp.einsum('bsk,bkd->bsd', _ctx_2048c, _ctx_2048P)
        _ctx_2048t = _ctx_2048t * jax.lax.rsqrt(jnp.mean(jnp.square(_ctx_2048t)) + 1e-12) * 0.953939
        ctx_2048 = 4.13588e-05 + 0.999923 * (_ctx_2048t + 0.3 * jax.random.normal(jax.random.fold_in(_rk, 611), (4, 512, 512), jnp.float32))
        return (x, ctx_2048)
    x, ctx_2048 = _rec_inputs()

    def _L0_attn_setup():
        import jax, jax.numpy as jnp
        import numpy as np
        D_MODEL = 512
        N_HEADS = 16
        D_HEAD = D_MODEL // N_HEADS
        B, S = (2, 512)
        EPS = 1e-05

        def _mhsa(X, ln_g, ln_b, Wq, bq, Wk, bk, Wv, bv, Wo, bo):
            n_ctx = X.shape[-2]
            mu = jnp.mean(X, axis=-1, keepdims=True)
            var = jnp.mean(jnp.square(X - mu), axis=-1, keepdims=True)
            Xn = (X - mu) * jax.lax.rsqrt(var + EPS) * ln_g + ln_b

            def split_heads(t):
                return t.reshape(t.shape[:-1] + (N_HEADS, D_HEAD)).swapaxes(-2, -3)
            Q = split_heads(Xn @ Wq + bq)
            K = split_heads(Xn @ Wk + bk)
            V = split_heads(Xn @ Wv + bv)
            scores = jnp.einsum('bhqd,bhkd->bhqk', Q, K) / jnp.sqrt(jnp.float32(D_HEAD))
            causal = jnp.tril(jnp.ones((n_ctx, n_ctx), dtype=bool))
            scores = jnp.where(causal, scores, jnp.float32(-jnp.inf))
            A = jax.nn.softmax(scores, axis=-1)
            AV = jnp.einsum('bhqk,bhkd->bhqd', A, V)
            AV = AV.swapaxes(-2, -3).reshape(X.shape[:-1] + (D_MODEL,))
            return AV @ Wo + bo
        key = jax.random.key(seed)
        ks = jax.random.split(key, 10)
        sd = 1.0 / np.sqrt(D_MODEL)
        inp = {'X': jax.random.normal(ks[0], (B, S, D_MODEL), dtype=jnp.float32), 'ln_g': jnp.ones((D_MODEL,), jnp.float32), 'ln_b': jnp.zeros((D_MODEL,), jnp.float32), 'Wq': jax.random.uniform(ks[1], (D_MODEL, D_MODEL), jnp.float32, -sd, sd), 'bq': jax.random.uniform(ks[2], (D_MODEL,), jnp.float32, -sd, sd), 'Wk': jax.random.uniform(ks[3], (D_MODEL, D_MODEL), jnp.float32, -sd, sd), 'bk': jax.random.uniform(ks[4], (D_MODEL,), jnp.float32, -sd, sd), 'Wv': jax.random.uniform(ks[5], (D_MODEL, D_MODEL), jnp.float32, -sd, sd), 'bv': jax.random.uniform(ks[6], (D_MODEL,), jnp.float32, -sd, sd), 'Wo': jax.random.uniform(ks[7], (D_MODEL, D_MODEL), jnp.float32, -sd, sd), 'bo': jax.random.uniform(ks[8], (D_MODEL,), jnp.float32, -sd, sd)}
        return inp
    _L0_attn_all = _L0_attn_setup()
    _L0_attn_in = {k: v for k, v in _L0_attn_all.items() if k in ('ln_g', 'ln_b', 'Wq', 'bq', 'Wk', 'bk', 'Wv', 'bv', 'Wo', 'bo')}
    del _L0_attn_all

    def _L0_xattn_setup():
        import math
        import jax, jax.numpy as jnp
        import numpy as np
        HEADS = 16
        MASKED_BIAS = -10000.0

        def _mha(q, k, v):
            B, Sq, D = q.shape
            Sk = k.shape[-2]
            hd = D // HEADS
            qh = q.reshape(B, Sq, HEADS, hd).transpose(0, 2, 1, 3)
            kh = k.reshape(B, Sk, HEADS, hd).transpose(0, 2, 1, 3)
            vh = v.reshape(B, Sk, HEADS, hd).transpose(0, 2, 1, 3)
            scores = jnp.einsum('bhqd,bhkd->bhqk', qh, kh) / math.sqrt(hd)
            qi = jnp.arange(Sq)[:, None] + (Sk - Sq)
            ki = jnp.arange(Sk)[None, :]
            causal = ki <= qi
            scores = jnp.where(causal[None, None], scores, jnp.asarray(MASKED_BIAS, scores.dtype))
            attn = jax.nn.softmax(scores, axis=-1)
            out = jnp.einsum('bhqk,bhkd->bhqd', attn, vh)
            return out.transpose(0, 2, 1, 3).reshape(B, Sq, D)
        key = jax.random.key(seed)
        kq, kk, kv = jax.random.split(key, 3)
        B, S, D = (4, 256, 512)
        q = jax.random.normal(kq, (B, S, D), dtype=jnp.float32)
        k = jax.random.normal(kk, (B, S, D), dtype=jnp.float32)
        v = jax.random.normal(kv, (B, S, D), dtype=jnp.float32)
        return {'q': q, 'k': k, 'v': v}
    _L0_xattn_all = _L0_xattn_setup()
    _L0_xattn_in = {k: v for k, v in _L0_xattn_all.items() if k in ()}
    del _L0_xattn_all

    def _L0_ffn_setup():
        import jax, jax.numpy as jnp
        import numpy as np
        B, S, D = (2, 512, 512)
        E, I, TOPK = (64, 192, 8)
        M = B * S
        CAP = 2 * (M * TOPK) // E

        def _moe(x, router_weight, gate_proj, up_proj, down_proj):
            b, s, d = x.shape
            xf = x.reshape(-1, d)
            m = xf.shape[0]
            logits = xf @ router_weight
            probs = jax.nn.softmax(logits.astype(jnp.float32), axis=-1)
            topw, topi = jax.lax.top_k(probs, TOPK)
            topw = topw / topw.sum(axis=-1, keepdims=True)
            flat_e = topi.reshape(-1)
            flat_w = topw.reshape(-1).astype(x.dtype)
            order = jnp.argsort(flat_e)
            se = flat_e[order]
            tok = order // TOPK
            counts = jax.ops.segment_sum(jnp.ones_like(flat_e), flat_e, num_segments=E)
            starts = jnp.cumsum(counts) - counts
            pos = jnp.arange(m * TOPK) - starts[se]
            valid = pos < CAP
            posc = jnp.minimum(pos, CAP - 1)
            xe = jnp.zeros((E, CAP, d), x.dtype).at[se, pos].set(xf[tok], mode='drop')
            h = jax.nn.silu(jnp.einsum('ecd,edi->eci', xe, gate_proj)) * jnp.einsum('ecd,edi->eci', xe, up_proj)
            ye = jnp.einsum('eci,eid->ecd', h, down_proj)
            contrib = jnp.where(valid[:, None], ye[se, posc], 0.0) * flat_w[order][:, None]
            out = jnp.zeros((m, d), x.dtype).at[tok].add(contrib)
            return out.reshape(b, s, d)
        key = jax.random.key(seed)
        k0, k1, k2, k3, k4 = jax.random.split(key, 5)
        return {'x': jax.random.normal(k0, (B, S, D), jnp.float32), 'router_weight': jax.random.normal(k1, (D, E), jnp.float32) * 0.02, 'gate_proj': jax.random.normal(k2, (E, D, I), jnp.float32) * 0.02, 'up_proj': jax.random.normal(k3, (E, D, I), jnp.float32) * 0.02, 'down_proj': jax.random.normal(k4, (E, I, D), jnp.float32) * 0.02}
    _L0_ffn_all = _L0_ffn_setup()
    _L0_ffn_in = {k: v for k, v in _L0_ffn_all.items() if k in ('router_weight', 'gate_proj', 'up_proj', 'down_proj')}
    del _L0_ffn_all
    return {'x': x, 'ctx_2048': ctx_2048, 'L0_attn_ln_g': _L0_attn_in['ln_g'], 'L0_attn_ln_b': _L0_attn_in['ln_b'], 'L0_attn_Wq': _L0_attn_in['Wq'], 'L0_attn_bq': _L0_attn_in['bq'], 'L0_attn_Wk': _L0_attn_in['Wk'], 'L0_attn_bk': _L0_attn_in['bk'], 'L0_attn_Wv': _L0_attn_in['Wv'], 'L0_attn_bv': _L0_attn_in['bv'], 'L0_attn_Wo': _L0_attn_in['Wo'], 'L0_attn_bo': _L0_attn_in['bo'], 'L0_ffn_router_weight': _L0_ffn_in['router_weight'], 'L0_ffn_gate_proj': _L0_ffn_in['gate_proj'], 'L0_ffn_up_proj': _L0_ffn_in['up_proj'], 'L0_ffn_down_proj': _L0_ffn_in['down_proj']}

def reference(x, ctx_2048, L0_attn_ln_g, L0_attn_ln_b, L0_attn_Wq, L0_attn_bq, L0_attn_Wk, L0_attn_bk, L0_attn_Wv, L0_attn_bv, L0_attn_Wo, L0_attn_bo, L0_ffn_router_weight, L0_ffn_gate_proj, L0_ffn_up_proj, L0_ffn_down_proj):
    import jax
    import jax.numpy as jnp

    def _L0_attn_ref(X, ln_g, ln_b, Wq, bq, Wk, bk, Wv, bv, Wo, bo):
        import jax, jax.numpy as jnp
        import numpy as np
        D_MODEL = 512
        N_HEADS = 16
        D_HEAD = D_MODEL // N_HEADS
        B, S = (2, 512)
        EPS = 1e-05

        def _mhsa(X, ln_g, ln_b, Wq, bq, Wk, bk, Wv, bv, Wo, bo):
            n_ctx = X.shape[-2]
            mu = jnp.mean(X, axis=-1, keepdims=True)
            var = jnp.mean(jnp.square(X - mu), axis=-1, keepdims=True)
            Xn = (X - mu) * jax.lax.rsqrt(var + EPS) * ln_g + ln_b

            def split_heads(t):
                return t.reshape(t.shape[:-1] + (N_HEADS, D_HEAD)).swapaxes(-2, -3)
            Q = split_heads(Xn @ Wq + bq)
            K = split_heads(Xn @ Wk + bk)
            V = split_heads(Xn @ Wv + bv)
            scores = jnp.einsum('bhqd,bhkd->bhqk', Q, K) / jnp.sqrt(jnp.float32(D_HEAD))
            causal = jnp.tril(jnp.ones((n_ctx, n_ctx), dtype=bool))
            scores = jnp.where(causal, scores, jnp.float32(-jnp.inf))
            A = jax.nn.softmax(scores, axis=-1)
            AV = jnp.einsum('bhqk,bhkd->bhqd', A, V)
            AV = AV.swapaxes(-2, -3).reshape(X.shape[:-1] + (D_MODEL,))
            return AV @ Wo + bo
        return _mhsa(X, ln_g, ln_b, Wq, bq, Wk, bk, Wv, bv, Wo, bo)

    def _L0_xattn_ref(q, k, v):
        import math
        import jax, jax.numpy as jnp
        import numpy as np
        HEADS = 16
        MASKED_BIAS = -10000.0

        def _mha(q, k, v):
            B, Sq, D = q.shape
            Sk = k.shape[-2]
            hd = D // HEADS
            qh = q.reshape(B, Sq, HEADS, hd).transpose(0, 2, 1, 3)
            kh = k.reshape(B, Sk, HEADS, hd).transpose(0, 2, 1, 3)
            vh = v.reshape(B, Sk, HEADS, hd).transpose(0, 2, 1, 3)
            scores = jnp.einsum('bhqd,bhkd->bhqk', qh, kh) / math.sqrt(hd)
            qi = jnp.arange(Sq)[:, None] + (Sk - Sq)
            ki = jnp.arange(Sk)[None, :]
            causal = ki <= qi
            scores = jnp.where(causal[None, None], scores, jnp.asarray(MASKED_BIAS, scores.dtype))
            attn = jax.nn.softmax(scores, axis=-1)
            out = jnp.einsum('bhqk,bhkd->bhqd', attn, vh)
            return out.transpose(0, 2, 1, 3).reshape(B, Sq, D)
        return _mha(q, k, v)

    def _L0_ffn_ref(x, router_weight, gate_proj, up_proj, down_proj):
        import jax, jax.numpy as jnp
        import numpy as np
        B, S, D = (2, 512, 512)
        E, I, TOPK = (64, 192, 8)
        M = B * S
        CAP = 2 * (M * TOPK) // E

        def _moe(x, router_weight, gate_proj, up_proj, down_proj):
            b, s, d = x.shape
            xf = x.reshape(-1, d)
            m = xf.shape[0]
            logits = xf @ router_weight
            probs = jax.nn.softmax(logits.astype(jnp.float32), axis=-1)
            topw, topi = jax.lax.top_k(probs, TOPK)
            topw = topw / topw.sum(axis=-1, keepdims=True)
            flat_e = topi.reshape(-1)
            flat_w = topw.reshape(-1).astype(x.dtype)
            order = jnp.argsort(flat_e)
            se = flat_e[order]
            tok = order // TOPK
            counts = jax.ops.segment_sum(jnp.ones_like(flat_e), flat_e, num_segments=E)
            starts = jnp.cumsum(counts) - counts
            pos = jnp.arange(m * TOPK) - starts[se]
            valid = pos < CAP
            posc = jnp.minimum(pos, CAP - 1)
            xe = jnp.zeros((E, CAP, d), x.dtype).at[se, pos].set(xf[tok], mode='drop')
            h = jax.nn.silu(jnp.einsum('ecd,edi->eci', xe, gate_proj)) * jnp.einsum('ecd,edi->eci', xe, up_proj)
            ye = jnp.einsum('eci,eid->ecd', h, down_proj)
            contrib = jnp.where(valid[:, None], ye[se, posc], 0.0) * flat_w[order][:, None]
            out = jnp.zeros((m, d), x.dtype).at[tok].add(contrib)
            return out.reshape(b, s, d)
        return _moe(x, router_weight, gate_proj, up_proj, down_proj)
    x = _layernorm(x + _L0_attn_ref(x, L0_attn_ln_g, L0_attn_ln_b, L0_attn_Wq, L0_attn_bq, L0_attn_Wk, L0_attn_bk, L0_attn_Wv, L0_attn_bv, L0_attn_Wo, L0_attn_bo), axis=-1)
    x = _layernorm(x + _L0_xattn_ref(x, ctx_2048, ctx_2048), axis=-1)
    x = _layernorm(x + _L0_ffn_ref(x, L0_ffn_router_weight, L0_ffn_gate_proj, L0_ffn_up_proj, L0_ffn_down_proj), axis=-1)
    return x

_drawn_inputs = setup_inputs


def setup_inputs(seed=0):
    import zlib

    import numpy as np

    out = dict(_drawn_inputs(seed))
    spreads = {'L0_attn_ln_g': (1.0, 0.6), 'L0_attn_ln_b': (0.0, 0.268)}
    factors = {'L0_attn_Wq': 4.464,
     'L0_attn_bq': 8.0,
     'L0_attn_Wk': 4.437,
     'L0_attn_bk': 8.0,
     'L0_attn_bv': 4.079,
     'L0_ffn_router_weight': 5.938,
     'L0_ffn_gate_proj': 5.685,
     'L0_ffn_up_proj': 5.592,
     'L0_ffn_down_proj': 5.583}
    for name, (base, spread) in spreads.items():
        noise = np.random.default_rng([zlib.crc32(name.encode()), seed]).standard_normal(out[name].shape)
        drawn = base * np.exp(spread * noise) if base else spread * noise
        out[name] = jnp.asarray(drawn.astype(out[name].dtype))
    for name, factor in factors.items():
        out[name] = (out[name] * factor).astype(out[name].dtype)
    return out
```

```python
from contextlib import ExitStack

import concourse.bass as bass
from concourse import mybir

F32 = mybir.dt.float32
F32R = mybir.dt.float32r
BF16 = mybir.dt.bfloat16
I32 = mybir.dt.int32
ALU = mybir.AluOpType
ACT = mybir.ActivationFunctionType
AX = mybir.AxisListType

P = 128
B, S, D = 4, 512, 512
H, DH = 16, 32
NC_ = D // P
NT = S // P
HG = P // DH
E, I, TOPK = 64, 192, 8
CAP = 2 * (2 * 512 * TOPK) // E
TOK = B * S
SLOTS = E * CAP
XROW = D + E
EPS = 1e-5
SCALE = float(DH) ** -0.5
MASKED = -1.0e30
MASKED_BIAS = 10000.0
BIG = 3.0e38
HEADS = NC_ * NT * HG
UNITS = NC_ * NT
TURNED = 8
PRIME = 64


def attention_steps(a):
    per_group = NT * HG
    for i in range(HEADS + 6):
        if i < HEADS:
            yield ("scores", a, i)
        if 2 <= i < HEADS + 2:
            yield ("probsT", a, i - 2)
        if 3 <= i < HEADS + 3 and (i - 3) % HG == HG - 1:
            unit = (i - 3) // HG
            yield ("values", a, unit)
            if unit % NT == NT - 1:
                yield ("outcopy", a, unit // NT)
        if 5 <= i < HEADS + 5 and (i - 5) % per_group == per_group - 1:
            yield ("outT", a, (i - 5) // per_group)
            yield ("normalize", a, (i - 5) // per_group)
        if i % per_group == 4 and i // per_group < NC_ - 1:
            g = i // per_group + 1
            yield ("q", a, g)
            yield ("k", a, g)


def batch_steps():
    yield from (("xT", 0, c) for c in range(NC_))
    yield from (("q", 0, 0), ("k", 0, 0))
    yield from (("v", 0, t) for t in range(NT))
    yield from attention_steps(0)
    yield from (("oT", 0, g) for g in range(NC_))
    yield from (("proj", 0, t) for t in range(NT))
    yield from (("suffix", 1, t) for t in range(NT))
    yield ("norm1", 0, 0)
    yield from (("q", 1, 0), ("k", 1, 0))
    yield from attention_steps(1)
    yield ("norm2", 1, 0)
    yield from (("x2T", 1, t) for t in range(NT))
    yield ("logits", 1, 0)
    yield ("places", 1, 0)


STEPS = list(batch_steps())
RING = 3
USERS = [s for s in STEPS if s[0] in
         ("xT", "q", "k", "v", "probsT", "outT", "oT", "proj", "suffix", "x2T", "logits", "places")]
RING_USE = {s: n for n, s in enumerate(USERS)}
PER_BANK = [len([n for n in range(len(USERS)) if n % RING == r]) for r in range(RING)]
STACK_INC = 16 * 2 * 3 * HG


def kernel_body(nc, x, ctx_in, ln_g, ln_b, Wq, bq, Wk, bk, Wv, bv, Wo, bo, Wr, gate_up, down, out):
    xg = nc.dram_tensor("x2_and_gates", [TOK + CAP, XROW], F32).ap()
    acc = nc.dram_tensor("residual_sum", [TOK + CAP, D], F32).ap()
    table = nc.dram_tensor("slot_token", [SLOTS, 1], I32).ap()
    attention_phase(nc, x, ctx_in, ln_g, ln_b, Wq, bq, Wk, bk, Wv, bv, Wo, bo, Wr, xg, acc, table)
    expert_phase(nc, gate_up, down, xg, acc, table)
    final_phase(nc, acc, out)


def attention_phase(nc, x, ctx_in, ln_g, ln_b, Wq, bq, Wk, bk, Wv, bv, Wo, bo, Wr, xg, acc, table):
    with ExitStack() as ctx:
        def sb(name, shape, dt=F32):
            return ctx.enter_context(nc.sbuf_tensor(name, shape, dt))

        def sem(name):
            return ctx.enter_context(nc.semaphore(name))

        xin = sb("xin", [P, NT, D])
        ctxv = sb("ctxv", [P, NT, D])
        x1 = sb("x1", [P, NT, D])
        o_sb = sb("o_sb", [P, NT, D])
        vals = sb("vals", [P, NT, D])
        suffix = vals
        xT_hi = sb("xT_hi", [P, NC_, S], F32R)
        xT_lo = sb("xT_lo", [P, NC_, S], F32R)
        w_hi = [sb(f"w_hi{i}", [P, NC_, D], F32R) for i in range(4)]
        w_lo = [sb(f"w_lo{i}", [P, NC_, D], F32R) for i in range(4)]
        part = {(w, p): sb(f"part_{w}_{p}", [P, S], F32R) for w in "qk" for p in ("hi", "lo")}
        stack = {(w, i): sb(f"stack_{w}{i}", [3 * DH, HG, S], F32R) for w in "qk" for i in range(2)}
        v_tmp = sb("v_tmp", [P, S])
        probs = [sb(f"probs{i}", [P, S]) for i in range(3)]
        probsT = [sb(f"probsT{i}", [P, S]) for i in range(TURNED)]
        outT = sb("outT", [P, S])
        mask = sb("mask", [P, S])
        neg_max = [sb(f"neg_max{i}", [P, NT, HG]) for i in range(2)]
        denom = [sb(f"denom{i}", [P, NT, HG]) for i in range(2)]
        rdenom = sb("rdenom", [P, NT, HG])
        e_mask = sb("e_mask", [P, NT, HG])
        e_cnt = sb("e_cnt", [P, NT, HG])
        tail = sb("tail", [P, NT, P])
        behind = sb("behind", [P, NT])
        least = sb("least", [P, 2])
        ident = sb("ident", [P, P])
        tri = sb("tri", [P, P])
        ones = sb("ones", [P, P])
        tri_before = sb("tri_before", [P, P], BF16)
        ones_bf = sb("ones_bf", [P, P], BF16)
        gcol = sb("gcol", [P, NC_])
        bcol = sb("bcol", [P, NC_])
        bqcol = sb("bqcol", [P, NC_])
        bkcol = sb("bkcol", [P, NC_])
        bv_rows = sb("bv_rows", [P, D])
        bo_rows = sb("bo_rows", [P, D])
        wr_sb = sb("wr_sb", [P, NC_, E])
        minus_bias = sb("minus_bias", [P, 1])
        stats = sb("stats", [P, NT, 6])
        mv = sb("mv", [P, NT, 2])
        var = sb("var", [P, NT])
        rstd = sb("rstd", [P, NT])
        power = sb("power", [P, NT])
        logit = sb("logit", [P, NT, E])
        left = sb("left", [P, NT, E])
        chosen = sb("chosen", [P, NT, E])
        chosen_bf = sb("chosen_bf", [P, NT, E], BF16)
        chosen_sum = sb("chosen_sum", [P, E], BF16)
        gates = sb("gates", [P, NT, E])
        top = sb("top", [P, NT, TOPK])
        neg_top = sb("neg_top", [P, NT])
        gsum = sb("gsum", [P, NT])
        rgsum = sb("rgsum", [P, NT])
        place = sb("place", [P, NT, E])
        wrap = sb("wrap", [P, NT, E])
        col2e = sb("col2e", [P, NT, E])
        key8 = sb("key8", [P, NT, TOPK])
        gone8 = sb("gone8", [P, NT, TOPK])
        slot8 = sb("slot8", [P, NT, TOPK], I32)
        ids_all = sb("ids_all", [P, B, NT], I32)
        ids = sb("ids", [P, NT], I32)
        pad_ids = sb("pad_ids", [P, P], I32)

        s_bank = [ctx.enter_context(nc.psum_tensor(f"s_bank{i}", [P, 512], F32)) for i in range(4)]
        ring = [ctx.enter_context(nc.psum_tensor(f"ring{i}", [P, 512], F32)) for i in range(RING)]
        o_bank = ctx.enter_context(nc.psum_tensor("o_bank", [P, S], F32))

        consts_loaded = sem("consts_loaded")
        w_loaded = sem("w_loaded")
        pool_ready = sem("pool_ready")
        dve_ready = sem("dve_ready")
        x_loaded = sem("x_loaded")
        ctx_loaded = sem("ctx_loaded")
        x_used = sem("x_used")
        ctx_used = sem("ctx_used")
        filled = sem("filled")
        freed = [sem(f"freed{r}") for r in range(RING)]
        scored = sem("scored")
        maxed = sem("maxed")
        exped = sem("exped")
        pv_done = sem("pv_done")
        o_copied = sem("o_copied")
        o_normed = sem("o_normed")
        part_hi = sem("part_hi")
        xt_hi = sem("xt_hi")
        xt_ready = sem("xt_ready")
        stacked = [sem(f"stacked{i}") for i in range(2)]
        e_ready = sem("e_ready")
        stat_ready = sem("stat_ready")
        settled = sem("settled")
        rstd_step = sem("rstd_step")
        rstd_ready = sem("rstd_ready")
        normed = sem("normed")
        res_ready = sem("res_ready")
        x1_used = sem("x1_used")
        logits_ready = sem("logits_ready")
        gexp_ready = sem("gexp_ready")
        chosen_ready = sem("chosen_ready")
        routed = sem("routed")
        ids_ready = sem("ids_ready")
        x2_stored = sem("x2_stored")
        tokens_stored = sem("tokens_stored")
        slots_free = sem("slots_free")
        init_stored = sem("init_stored")

        INIT_STORES = 16 * (1 + 4 * (CAP // P))

        def ring_use(step):
            n = RING_USE[step]
            return n, n % RING, n // RING

        def last_uses(steps):
            uses = [ring_use(step)[1:] for step in steps]
            return [(r, max(k for s, k in uses if s == r)) for r in sorted({r for r, _ in uses})]

        def wait_filled(eng, b, step):
            eng.wait_ge(filled, b * len(USERS) + (RING_USE[step] + 1))

        def tiles_of(src, b):
            return src[bass.ds(b, 1), :, :].rearrange("a (t p) d -> (a p) t d", p=P)

        def settle(eng):
            eng.sem_inc(settled, 1)

        def stack_use(a, g):
            u = a * NC_ + g
            return u % 2, u // 2

        block = ctx.enter_context(nc.Block())

        @block.sync
        def _(sp):
            with nc.allow_non_contiguous_dma(reason="a few vectors laid along partitions"):
                for vec, col in ((ln_g, gcol), (ln_b, bcol), (bq, bqcol), (bk, bkcol)):
                    sp.dma_start(col[:, :], vec.rearrange("(c p) -> p c", p=P)).then_inc(consts_loaded, 16)
                sp.dma_start(bv_rows[:, :], bv.rearrange("(a n) -> a n", a=1).to_broadcast([P, D])).then_inc(consts_loaded, 16)
                sp.dma_start(bo_rows[:, :], bo.rearrange("(a n) -> a n", a=1).to_broadcast([P, D])).then_inc(consts_loaded, 16)
                sp.dma_start(wr_sb[:, :, :], Wr.rearrange("(c p) e -> p c e", p=P)).then_inc(consts_loaded, 16)
            for w, buf in ((Wq, ctxv), (Wk, x1), (Wv, vals), (Wo, o_sb)):
                sp.dma_start(buf[:, :, :], w.rearrange("(c p) n -> p c n", p=P)).then_inc(w_loaded, 16)
            sp.wait_ge(pool_ready, 2)
            sp.dma_start(table.rearrange("(p n) a -> p (n a)", p=P), pad_ids[:, :]).then_inc(init_stored, 16)
            for h in range(CAP // P):
                rows = slice(TOK + h * P, TOK + (h + 1) * P)
                for dst, width in ((xg, XROW), (acc, D)):
                    sp.dma_start(dst[rows, 0:S - P], mask[:, 0:S - P]).then_inc(init_stored, 16)
                    sp.dma_start(dst[rows, S - P:width], mask[:, 0:width - (S - P)]).then_inc(init_stored, 16)

            def load_x(b):
                sp.wait_ge(x_used, b + 1)
                sp.dma_start(xin[:, :, :], tiles_of(x, b)).then_inc(x_loaded, 16)

            def batch(b, last):
                sp.wait_ge(ctx_used, b + 1)
                settle(sp)
                sp.dma_start(ctxv[:, :, :], tiles_of(ctx_in, b)).then_inc(ctx_loaded, 16)
                for a in range(2):
                    for g in range(NC_):
                        buf, n = stack_use(a, g)
                        sp.wait_ge(scored, b * (2 * HEADS) + ((a * NC_ + g - 1) * NT * HG + PRIME))
                        settle(sp)
                        for w, order in (("q", ("hi", "hi", "lo")), ("k", ("hi", "lo", "hi"))):
                            settle(sp)
                            _, r, k = ring_use((w, a, g))
                            sp.wait_ge(freed[r], b * PER_BANK[r] + (k + 1 + PRIME))
                            settle(sp)
                            for q, p in enumerate(order):
                                for j in range(HG):
                                    sp.dma_start(stack[w, buf][DH * q:DH * (q + 1), j, :].bitcast(F32),
                                                 part[w, p][DH * j:DH * (j + 1), :].bitcast(F32)).then_inc(stacked[buf], 16)
                    if a == 0 and not last:
                        load_x(b + 1)
                sp.wait_ge(normed, b * 3 + 3)
                sp.wait_ge(routed, b + 1)
                for t in range(NT):
                    row = b * S + t * P
                    sp.dma_start(xg[bass.ds(row, P), 0:D], o_sb[:, t, :]).then_inc(x2_stored, 16)
                    sp.dma_start(acc[bass.ds(row, P), :], o_sb[:, t, :]).then_inc(x2_stored, 16)
                    sp.dma_start(xg[bass.ds(row, P), D:XROW], gates[:, t, :]).then_inc(x2_stored, 16)

            load_x(0)
            with sp.Fori(0, B - 1) as b:
                batch(b, last=False)
            batch(B - 1, last=True)
            sp.wait_ge(x2_stored, B * NT * 48 + PRIME)
            sp.wait_ge(init_stored, INIT_STORES)

        @block.gpsimd
        def _(pool):
            pool.iota(pad_ids[:, :], [[0, E], [P, 2]], base=TOK, channel_multiplier=1).then_inc(pool_ready, 1)
            for buf, v in ((ident, 0.0), (tri, 1.0), (ones, 1.0), (mask, 0.0), (tri_before, 1.0),
                           (ones_bf, 1.0), (power, -0.5), (minus_bias, -MASKED_BIAS), (chosen_sum, 0.0)):
                pool.memset(buf[:, :], v)
            pool.memset(least[:, :], MASKED_BIAS)
            pool.iota(ids_all[:, :, :], [[S, B], [P, NT]], base=0, channel_multiplier=1)
            pool.iota(col2e[:, :, :], [[0, NT], [2, E]], base=1, channel_multiplier=0,
                      allow_small_or_imprecise_dtypes=True)
            pool.iota(behind[:, :], [[-P, NT]], base=S - 1, channel_multiplier=-1,
                      allow_small_or_imprecise_dtypes=True).then_inc(pool_ready, 1)
            pool.wait_ge(pool_ready, 2)
            pool.affine_select(out=ident[:, :], in_=ident[:, :], compare_op=ALU.not_equal, fill=1.0,
                               base=0, pattern=[[-1, P]], channel_multiplier=1)
            pool.affine_select(out=tri[:, :], in_=tri[:, :], compare_op=ALU.is_gt, fill=0.0,
                               base=0, pattern=[[-1, P]], channel_multiplier=1)
            pool.affine_select(out=tri_before[:, :], in_=tri_before[:, :], compare_op=ALU.is_gt, fill=0.0,
                               base=0, pattern=[[1, P]], channel_multiplier=-1)
            pool.affine_select(out=mask[:, S - P:S], in_=mask[:, S - P:S], compare_op=ALU.is_ge, fill=MASKED,
                               base=0, pattern=[[-1, P]], channel_multiplier=1)
            pool.affine_select(out=least[:, 1:2], in_=least[:, 1:2], compare_op=ALU.is_gt, fill=BIG,
                               base=P - 1, pattern=[[0, 1]], channel_multiplier=-1).then_inc(pool_ready, 1)
            pool.wait_ge(init_stored, INIT_STORES)

            def inverse_deviation(b, n):
                pool.wait_ge(stat_ready, b * 3 + (n + 1))
                settle(pool)
                pool.tensor_scalar(var[:, :], mv[:, :, 1], EPS, 0.0, ALU.add, ALU.add).then_inc(rstd_step, 1)
                pool.wait_ge(rstd_step, b * 3 + (n + 1))
                pool.tensor_tensor(rstd[:, :], var[:, :], power[:, :], ALU.pow).then_inc(rstd_ready, 1)

            pool.wait_ge(consts_loaded, 16 * 7)

            def batch(b, last):
                pool.wait_ge(x1_used, b + 1)
                pool.wait_ge(x_loaded, b * 16 + 16)
                for t in range(NT):
                    add = pool.tensor_tensor(x1[:, t, :], xin[:, t, :], bo_rows[:, :], ALU.add)
                add.then_inc(res_ready, 1)
                inverse_deviation(b, 1)
                inverse_deviation(b, 2)
                if not last:
                    inverse_deviation(b + 1, 0)
                pool.wait_ge(routed, b + 1)
                settle(pool)
                pool.tensor_copy(ids[:, :], ids_all[:, bass.ds(b, 1), :].rearrange("p a t -> p (a t)")).then_inc(ids_ready, 1)
                pool.wait_ge(ids_ready, b + 1)
                settle(pool)
                for t in range(NT):
                    for j in range(TOPK):
                        pool.indirect_dma_start(
                            table, bass.IndirectOffsetOnAxis(ap=slot8[:, t, j:j + 1], axis=0), ids[:, t:t + 1], None,
                            bounds_check=SLOTS - 1, oob_is_err=False).then_inc(tokens_stored, 16)
                pool.wait_ge(tokens_stored, (b + 1) * (16 * NT * TOPK))
                pool.sem_inc(slots_free, 1)

            pool.sem_inc(slots_free, 1)
            inverse_deviation(0, 0)
            with pool.Fori(0, B - 1) as b:
                batch(b, last=False)
            batch(B - 1, last=True)

        @block.tensor
        def _(pe):
            pe.sem_inc(scored, PRIME)
            pe.wait_ge(pool_ready, 3)
            pe.wait_ge(consts_loaded, 16 * 7)
            pe.wait_ge(dve_ready, 5)

            def bank_free(b, step):
                _, r, k = ring_use(step)
                pe.wait_ge(freed[r], b * PER_BANK[r] + (k + PRIME))
                return ring[r]

            def three_passes(dst, pairs):
                ops = [(s, m) for s_hi, s_lo, m_hi, m_lo in pairs for s, m in ((s_hi, m_hi), (s_hi, m_lo), (s_lo, m_hi))]
                for i, (s, m) in enumerate(ops):
                    last = nc.tensor.matmul(dst, s, m, start=(i == 0), stop=(i == len(ops) - 1))
                return last

            def transposed(b, step, blocks):
                bank = bank_free(b, step)
                for i, src in enumerate(blocks):
                    last = nc.tensor.transpose(bank[:, P * i:P * (i + 1)], src, ident[:, :])
                last.then_inc(filled, 1)

            with pe.Fori(0, B) as b:
                for step in STEPS:
                    kind, a, n = step
                    if kind == "xT":
                        if n == 0:
                            pe.wait_ge(normed, b * 3 + 1)
                        transposed(b, step, [o_sb[:, t, n * P:(n + 1) * P] for t in range(NT)])
                    elif kind in "qk" and a == 0:
                        if n == 0 and kind == "q":
                            pe.wait_ge(xt_ready, b * (2 * NC_) + NC_)
                        bank = bank_free(b, step)
                        w = 0 if kind == "q" else 1
                        cols = slice(n * P, (n + 1) * P)
                        three_passes(bank[:, :], [(w_hi[w][:, c, cols], w_lo[w][:, c, cols], xT_hi[:, c, :], xT_lo[:, c, :])
                                                  for c in range(NC_)]).then_inc(filled, 1)
                    elif kind in "qk":
                        if kind == "k" and n == 0:
                            pe.wait_ge(ctx_loaded, b * 16 + 16)
                        src = x1 if kind == "q" else ctxv
                        transposed(b, step, [src[:, t, n * P:(n + 1) * P] for t in range(NT)])
                    elif kind == "v":
                        bank = bank_free(b, step)
                        rows = slice(n * P, (n + 1) * P)
                        three_passes(bank[:, :], [(xT_hi[:, c, rows], xT_lo[:, c, rows], w_hi[2][:, c, :], w_lo[2][:, c, :])
                                                  for c in range(NC_)]).then_inc(filled, 1)
                    elif kind == "scores":
                        g, qi, j = n // (NT * HG), n // HG % NT, n % HG
                        buf, k = stack_use(a, g)
                        if qi == 0 and j == 0:
                            pe.wait_ge(stacked[buf], b * (NC_ * STACK_INC) + (STACK_INC * (k + 1) + PRIME))
                        pe.wait_ge(exped, b * (2 * HEADS) + (a * HEADS + n - 3 + PRIME))
                        cols = P * (qi + 1)
                        nc.tensor.matmul(s_bank[n % 4][:, 0:cols], stack["q", buf][:, j, qi * P:(qi + 1) * P],
                                         stack["k", buf][:, j, 0:cols], start=True, stop=True).then_inc(scored, 1)
                    elif kind == "probsT":
                        qi = n // HG % NT
                        pe.wait_ge(exped, b * (2 * HEADS) + (a * HEADS + n + 1 + PRIME))
                        transposed(b, step, [probs[n % 3][:, kb * P:(kb + 1) * P] for kb in range(qi + 1)])
                    elif kind == "values":
                        g, qi = n // NT, n % NT
                        if qi == 0:
                            pe.wait_ge(o_copied, b * (2 * NC_) + (a * NC_ + g + PRIME))
                            if a == 0 and n == 0:
                                _, r, k = ring_use(("v", 0, NT - 1))
                                pe.wait_ge(freed[r], b * PER_BANK[r] + (k + 1 + PRIME))
                        for r, k in last_uses([("probsT", a, n * HG + j) for j in range(HG)]):
                            pe.wait_ge(freed[r], b * PER_BANK[r] + (k + 1 + PRIME))
                        v = vals if a == 0 else ctxv
                        for kb in range(qi + 1):
                            for j in range(HG):
                                h = g * HG + j
                                last = nc.tensor.matmul(o_bank[j * DH:(j + 1) * DH, qi * P:(qi + 1) * P], v[:, kb, h * DH:(h + 1) * DH],
                                                        probsT[(n * HG + j) % TURNED][:, kb * P:(kb + 1) * P],
                                                        start=(kb == 0), stop=(kb == qi), tile_position=(0, j * DH))
                        last.then_inc(pv_done, 1)
                    elif kind == "outT":
                        pe.wait_ge(o_copied, b * (2 * NC_) + (a * NC_ + n + 1 + PRIME))
                        transposed(b, step, [outT[:, t * P:(t + 1) * P] for t in range(NT)])
                    elif kind == "oT":
                        pe.wait_ge(o_normed, b * (2 * NC_) + (n + 1 + PRIME))
                        transposed(b, step, [o_sb[:, t, n * P:(n + 1) * P] for t in range(NT)])
                    elif kind == "proj":
                        if n == 0:
                            pe.wait_ge(xt_ready, b * (2 * NC_) + 2 * NC_)
                        bank = bank_free(b, step)
                        rows = slice(n * P, (n + 1) * P)
                        three_passes(bank[:, :], [(xT_hi[:, c, rows], xT_lo[:, c, rows], w_hi[3][:, c, :], w_lo[3][:, c, :])
                                                  for c in range(NC_)]).then_inc(filled, 1)
                    elif kind == "suffix":
                        if n == 0:
                            pe.wait_ge(ctx_loaded, b * 16 + 16)
                        bank = bank_free(b, step)
                        for kb in range(n, NT):
                            last = nc.tensor.matmul(bank[:, :], (tri if kb == n else ones)[:, :], ctxv[:, kb, :],
                                                    start=(kb == n), stop=(kb == NT - 1))
                        last.then_inc(filled, 1)
                    elif kind == "norm1":
                        pe.wait_ge(normed, b * 3 + 2)
                    elif kind == "norm2":
                        pe.wait_ge(normed, b * 3 + 3)
                    elif kind == "x2T":
                        transposed(b, step, [o_sb[:, n, c * P:(c + 1) * P] for c in range(NC_)])
                    elif kind == "logits":
                        for r, k in last_uses([("x2T", 1, t) for t in range(NT)]):
                            pe.wait_ge(freed[r], b * PER_BANK[r] + (k + 1 + PRIME))
                        bank = bank_free(b, step)
                        for t in range(NT):
                            for c in range(NC_):
                                last = nc.tensor.matmul(bank[:, E * t:E * (t + 1)], suffix[:, t, c * P:(c + 1) * P],
                                                        wr_sb[:, c, :], start=(c == 0), stop=(c == NC_ - 1))
                        last.then_inc(filled, 1)
                    elif kind == "places":
                        pe.wait_ge(chosen_ready, b + 1)
                        bank = bank_free(b, step)
                        for t in range(NT):
                            nc.tensor.matmul(bank[:, E * t:E * (t + 1)], ones_bf[:, :], chosen_sum[:, :], start=True, stop=False)
                            for u in range(t):
                                nc.tensor.matmul(bank[:, E * t:E * (t + 1)], ones_bf[:, :], chosen_bf[:, u, :], start=False, stop=False)
                            last = nc.tensor.matmul(bank[:, E * t:E * (t + 1)], tri_before[:, :], chosen_bf[:, t, :],
                                                    start=False, stop=True)
                        last.then_inc(filled, 1)

        @block.scalar
        def _(act):
            act.sem_inc(exped, PRIME)
            act.sem_inc(o_copied, PRIME)
            act.sem_inc(stacked[0], PRIME)
            act.sem_inc(stacked[1], PRIME)
            act.sem_inc(x2_stored, PRIME)
            act.wait_ge(pool_ready, 3)
            act.wait_ge(consts_loaded, 16 * 7)
            with act.Fori(0, B) as b:
                for step in STEPS:
                    kind, a, n = step
                    bank = ring[ring_use(step)[1]] if step in RING_USE else None
                    free = freed[ring_use(step)[1]] if step in RING_USE else None
                    if kind == "xT":
                        wait_filled(act, b, step)
                        if n:
                            act.wait_ge(xt_ready, b * (2 * NC_) + n)
                        act.activation(v_tmp[:, :], bank[:, :], ACT.Identity, bias=bcol[:, n:n + 1],
                                       scale=gcol[:, n:n + 1]).then_inc(xt_hi, 1)
                    elif kind in "qk":
                        buf, k = stack_use(a, n)
                        prev = a * NC_ + n - 1
                        act.wait_ge(stacked[1 - buf], b * (NC_ * STACK_INC) + (STACK_INC * (prev // 2 + 1) + PRIME))
                        wait_filled(act, b, step)
                        if a == 0:
                            bias = (bqcol if kind == "q" else bkcol)[:, n:n + 1]
                            act.activation(part[kind, "hi"][:, :], bank[:, :], ACT.Identity, bias=bias).then_inc(part_hi, 1)
                        else:
                            act.activation(part[kind, "hi"][:, :], bank[:, :], ACT.Copy).then_inc(part_hi, 1)
                    elif kind == "scores":
                        g, qi, j = n // (NT * HG), n // HG % NT, n % HG
                        cols = P * (qi + 1)
                        act.wait_ge(maxed, b * (2 * HEADS) + (a * HEADS + n + 1))
                        if a or n >= 3:
                            before = ("probsT", a, n - 3) if n >= 3 else ("probsT", a - 1, HEADS + n - 3)
                            wait_filled(act, b, before)
                        act.activation(probs[n % 3][:, 0:cols], s_bank[n % 4][:, 0:cols], ACT.Exp,
                                       bias=neg_max[g % 2][:, qi, j:j + 1], scale=-1.0,
                                       accum_out=denom[g % 2][:, qi, j:j + 1]).then_inc(exped, 1)
                    elif kind == "probsT" and n % 2 == 1:
                        wait_filled(act, b, step)
                        if a or n >= TURNED:
                            act.wait_ge(pv_done, b * (2 * UNITS) + (a * UNITS + (n - TURNED) // HG + 1))
                        cols = P * (n // HG % NT + 1)
                        act.activation(probsT[n % TURNED][:, 0:cols], bank[:, 0:cols], ACT.Copy).then_inc(free, 1)
                    elif kind == "outcopy":
                        act.wait_ge(pv_done, b * (2 * UNITS) + (a * UNITS + NT * (n + 1)))
                        if a or n:
                            wait_filled(act, b, ("outT", a, n - 1) if n else ("outT", a - 1, NC_ - 1))
                        act.activation(outT[:, :], o_bank[:, :], ACT.Copy).then_inc(o_copied, 1)
                    elif kind == "normalize" and a == 1:
                        act.wait_ge(maxed, b * (2 * HEADS) + (HEADS + NT * HG * (n + 1)))
                        act.wait_ge(o_normed, b * (2 * NC_) + (NC_ + n + PRIME))
                        act.activation(e_mask[:, :, :], neg_max[n % 2][:, :, :], ACT.Exp, bias=minus_bias[:, 0:1]).then_inc(e_ready, 1)
                    elif kind == "oT":
                        wait_filled(act, b, step)
                        act.activation(xT_hi[:, n, :], bank[:, :], ACT.Copy).then_inc(xt_hi, 1)
                    elif kind == "suffix":
                        wait_filled(act, b, step)
                        act.activation(suffix[:, n, :], bank[:, :], ACT.Copy).then_inc(free, 1)
                    elif kind == "x2T":
                        wait_filled(act, b, step)
                        act.activation(suffix[:, n, :], bank[:, :], ACT.Copy).then_inc(free, 1)
                    elif kind == "logits":
                        act.wait_ge(logits_ready, b + 1)
                        for t in range(NT):
                            last = act.activation(gates[:, t, :], logit[:, t, :], ACT.Exp, bias=neg_top[:, t:t + 1])
                        last.then_inc(gexp_ready, 1)

        @block.vector
        def _(dve):
            for r in range(RING):
                dve.sem_inc(freed[r], PRIME)
            dve.sem_inc(o_normed, PRIME)
            dve.sem_inc(x_used, 1)
            dve.wait_ge(pool_ready, 3)
            dve.memset(v_tmp[:, 0:1], 0.0).then_inc(dve_ready, 1)
            dve.wait_ge(w_loaded, 64)
            for i, buf in enumerate((ctxv, x1, vals, o_sb)):
                dve.tensor_copy(w_hi[i][:, :, :], buf[:, :, :])
                dve.drain()
                dve.tensor_tensor(w_lo[i][:, :, :], buf[:, :, :], w_hi[i][:, :, :], ALU.subtract).then_inc(dve_ready, 1)
            dve.drain().then_inc(ctx_used, 1)
            dve.drain().then_inc(x1_used, 1)

            def moments(src, t):
                dve.bn_stats(stats[:, t, :], src[:, t, :])

            def layernorm(b, n, src, dst):
                dve.drain()
                for t in range(NT):
                    last = dve.bn_aggr(mv[:, t, :], stats[:, t, :])
                last.then_inc(stat_ready, 1)
                dve.wait_ge(rstd_ready, b * 3 + (n + 1))
                settle(dve)
                for t in range(NT):
                    last = dve.tensor_scalar(dst[:, t, :], src[:, t, :], mv[:, t, 0:1], rstd[:, t:t + 1],
                                             ALU.subtract, ALU.mult)
                last.then_inc(normed, 1)

            with dve.Fori(0, B) as b:
                dve.wait_ge(x_loaded, b * 16 + 16)
                for t in range(NT):
                    moments(xin, t)
                dve.wait_ge(x2_stored, b * (48 * NT) + PRIME)
                settle(dve)
                layernorm(b, 0, xin, o_sb)
                for step in STEPS:
                    kind, a, n = step
                    bank = ring[ring_use(step)[1]] if step in RING_USE else None
                    free = freed[ring_use(step)[1]] if step in RING_USE else None
                    if kind == "xT":
                        dve.wait_ge(xt_hi, b * (2 * NC_) + (n + 1))
                        dve.tensor_copy(xT_hi[:, n, :], v_tmp[:, :]).then_inc(free, 1)
                        dve.drain()
                        dve.tensor_tensor(xT_lo[:, n, :], v_tmp[:, :], xT_hi[:, n, :], ALU.subtract).then_inc(xt_ready, 1)
                    elif kind in "qk":
                        dve.wait_ge(part_hi, b * (4 * NC_) + (2 * (a * NC_ + n) + (kind == "k") + 1))
                        if a == 0:
                            bias = (bqcol if kind == "q" else bkcol)[:, n:n + 1]
                            dve.scalar_tensor_tensor(out=part[kind, "lo"][:, :], in0=bank[:, :], scalar=bias,
                                                     in1=part[kind, "hi"][:, :], op0=ALU.add, op1=ALU.subtract).then_inc(free, 1)
                        else:
                            dve.tensor_tensor(part[kind, "lo"][:, :], bank[:, :], part[kind, "hi"][:, :], ALU.subtract).then_inc(free, 1)
                    elif kind == "v":
                        wait_filled(dve, b, step)
                        dve.tensor_tensor(vals[:, n, :], bank[:, :], bv_rows[:, :], ALU.add).then_inc(free, 1)
                    elif kind == "scores":
                        g, qi, j = n // (NT * HG), n // HG % NT, n % HG
                        cols = P * (qi + 1)
                        s = s_bank[n % 4][:, 0:cols]
                        first = BIG if a == 0 else least[:, qi // (NT - 1):qi // (NT - 1) + 1]
                        dve.wait_ge(scored, b * (2 * HEADS) + (a * HEADS + n + 1 + PRIME))
                        settle(dve)
                        dve.tensor_tensor_reduce(s, s, mask[:, S - cols:S], -SCALE, first, ALU.add, ALU.min,
                                                 neg_max[g % 2][:, qi, j:j + 1]).then_inc(maxed, 1)
                    elif kind == "probsT" and n % 2 == 0:
                        wait_filled(dve, b, step)
                        if a or n >= TURNED:
                            dve.wait_ge(pv_done, b * (2 * UNITS) + (a * UNITS + (n - TURNED) // HG + 1))
                        cols = P * (n // HG % NT + 1)
                        dve.tensor_copy(probsT[n % TURNED][:, 0:cols], bank[:, 0:cols]).then_inc(free, 1)
                    elif kind == "normalize":
                        dst = o_sb[:, :, n * P:(n + 1) * P]
                        den = denom[n % 2]
                        use = ring_use(("outT", a, n))
                        free = freed[use[1]]
                        o_back = ring[use[1]][:, :].rearrange("p (t n) -> p t n", n=P)
                        wait_filled(dve, b, ("outT", a, n))
                        if a == 1:
                            dve.wait_ge(e_ready, b * NC_ + (n + 1))
                            settle(dve)
                            dve.tensor_tensor(e_cnt[:, :, :], e_mask[:, :, :],
                                              behind[:, :].unsqueeze(2).to_broadcast([P, NT, HG]), ALU.mult)
                            dve.tensor_tensor(tail[:, :, :].rearrange("p t (j d) -> p t j d", d=DH),
                                              suffix[:, :, n * P:(n + 1) * P].rearrange("p t (j d) -> p t j d", d=DH),
                                              e_mask[:, :, :].unsqueeze(3).to_broadcast([P, NT, HG, DH]), ALU.mult)
                            dve.drain()
                            dve.tensor_tensor(den[:, :, :], den[:, :, :], e_cnt[:, :, :], ALU.add)
                            dve.tensor_tensor(tail[:, :, :], o_back, tail[:, :, :], ALU.add).then_inc(free, 1)
                            dve.drain()
                        dve.reciprocal(rdenom[:, :, :], den[:, :, :])
                        dve.drain()
                        src = o_back if a == 0 else tail[:, :, :]
                        last = dve.tensor_tensor(dst.rearrange("p t (j d) -> p t j d", d=DH),
                                                 src.rearrange("p t (j d) -> p t j d", d=DH),
                                                 rdenom[:, :, :].unsqueeze(3).to_broadcast([P, NT, HG, DH]), ALU.mult)
                        if a == 0:
                            last.then_inc(free, 1)
                            dve.drain().then_inc(o_normed, 1)
                        else:
                            last.then_inc(o_normed, 1)
                            dve.drain()
                            dve.tensor_tensor(dst, dst, x1[:, :, n * P:(n + 1) * P], ALU.add)
                    elif kind == "oT":
                        dve.wait_ge(xt_hi, b * (2 * NC_) + (NC_ + n + 1))
                        dve.tensor_tensor(xT_lo[:, n, :], bank[:, :], xT_hi[:, n, :], ALU.subtract).then_inc(free, 1)
                        dve.drain().then_inc(xt_ready, 1)
                    elif kind == "proj":
                        if n == 0:
                            dve.wait_ge(res_ready, b + 1)
                            settle(dve)
                            dve.drain().then_inc(x_used, 1)
                        wait_filled(dve, b, step)
                        dve.tensor_tensor(x1[:, n, :], bank[:, :], x1[:, n, :], ALU.add).then_inc(free, 1)
                        dve.drain()
                        moments(x1, n)
                    elif kind == "norm1":
                        layernorm(b, 1, x1, x1)
                    elif kind == "norm2":
                        dve.drain().then_inc(x1_used, 1)
                        for t in range(NT):
                            moments(o_sb, t)
                        dve.drain().then_inc(ctx_used, 1)
                        layernorm(b, 2, o_sb, o_sb)
                    elif kind == "logits":
                        wait_filled(dve, b, step)
                        dve.tensor_copy(logit[:, :, :], bank[:, 0:NT * E].rearrange("p (t e) -> p t e", e=E)).then_inc(free, 1)
                        dve.drain()
                        for t in range(NT):
                            dve.max(top[:, t, :], logit[:, t, :])
                        dve.drain()
                        dve.tensor_scalar(neg_top[:, :], top[:, :, 0], -1.0, None, ALU.mult).then_inc(logits_ready, 1)
                        for t in range(NT):
                            dve.match_replace(left[:, t, :], top[:, t, :], logit[:, t, :], MASKED)
                        dve.drain()
                        dve.tensor_tensor(chosen[:, :, :], left[:, :, :], logit[:, :, :], ALU.not_equal)
                        dve.drain()
                        dve.tensor_copy(chosen_bf[:, :, :], chosen[:, :, :]).then_inc(chosen_ready, 1)
                        dve.wait_ge(gexp_ready, b + 1)
                        dve.tensor_tensor(gates[:, :, :], gates[:, :, :], chosen[:, :, :], ALU.mult)
                        dve.drain()
                        dve.tensor_reduce(gsum[:, :], gates[:, :, :], AX.X, ALU.add)
                        dve.drain()
                        dve.reciprocal(rgsum[:, :], gsum[:, :])
                        dve.drain()
                        for t in range(NT):
                            dve.tensor_scalar(gates[:, t, :], gates[:, t, :], rgsum[:, t:t + 1], None, ALU.mult)
                    elif kind == "places":
                        wait_filled(dve, b, step)
                        count = bank[:, 0:NT * E].rearrange("p (t e) -> p t e", e=E)
                        dve.tensor_scalar(wrap[:, :, :], count, float(P), -(P * P - 1.0), ALU.is_ge, ALU.mult)
                        dve.scalar_tensor_tensor(out=place[:, :, :], in0=count, scalar=float(P), in1=col2e[:, :, :],
                                                 op0=ALU.mult, op1=ALU.add)
                        dve.drain()
                        dve.tensor_tensor(place[:, :, :], place[:, :, :], wrap[:, :, :], ALU.add)
                        dve.scalar_tensor_tensor(out=chosen[:, :, :], in0=count, scalar=float(CAP), in1=chosen[:, :, :],
                                                 op0=ALU.is_lt, op1=ALU.mult).then_inc(free, 1)
                        for t in range(NT):
                            dve.tensor_tensor(chosen_sum[:, :], chosen_sum[:, :], chosen_bf[:, t, :], ALU.add)
                            dve.drain()
                        dve.tensor_tensor(place[:, :, :], place[:, :, :], chosen[:, :, :], ALU.mult)
                        dve.drain()
                        for t in range(NT):
                            dve.max(key8[:, t, :], place[:, t, :])
                        dve.drain()
                        dve.tensor_scalar(gone8[:, :, :], key8[:, :, :], 0.0, 65536.0, ALU.is_equal, ALU.mult)
                        dve.drain()
                        dve.wait_ge(slots_free, b + 1)
                        dve.scalar_tensor_tensor(out=slot8[:, :, :], in0=key8[:, :, :], scalar=-1.0, in1=gone8[:, :, :],
                                                 op0=ALU.add, op1=ALU.add).then_inc(routed, 1)


RT = CAP // P
MIX = I - P
GU = 2 * I
QUAD = 4


def expert_phase(nc, gate_up, down, xg, acc, table):
    with ExitStack() as ctx:
        def sb(name, shape, dt=F32):
            return ctx.enter_context(nc.sbuf_tensor(name, shape, dt))

        def sem(name):
            return ctx.enter_context(nc.semaphore(name))

        slots = sb("slots", [P, P], I32)
        idx = [sb(f"idx{i}", [P, RT], I32) for i in range(4)]
        xe = [sb(f"xe{i}", [P, RT, XROW]) for i in range(4)]
        gu = [sb(f"gu{i}", [P, NC_, GU]) for i in range(2)]
        gu_hi = [sb(f"gu_hi{i}", [P, NC_, GU], F32R) for i in range(2)]
        gu_lo = [sb(f"gu_lo{i}", [P, NC_, GU], F32R) for i in range(2)]
        dn = [sb(f"dn{i}", [P, 2, D]) for i in range(2)]
        dn_hi = [sb(f"dn_hi{i}", [P, 2, D], F32R) for i in range(2)]
        dn_lo = [sb(f"dn_lo{i}", [P, 2, D], F32R) for i in range(2)]
        xT_hi = [sb(f"exT_hi{i}", [P, NC_, CAP], F32R) for i in range(2)]
        xT_lo = [sb(f"exT_lo{i}", [P, NC_, CAP], F32R) for i in range(2)]
        silu = [sb(f"silu{i}", [P, 2, CAP]) for i in range(2)]
        h = [sb(f"h{i}", [P, 2, CAP]) for i in range(2)]
        h_hi = [sb(f"h_hi{i}", [P, 2, CAP], F32R) for i in range(2)]
        h_lo = [sb(f"h_lo{i}", [P, 2, CAP], F32R) for i in range(2)]
        y = [sb(f"y{i}", [P, RT, D]) for i in range(2)]
        ident = sb("eident", [P, P])

        ps_x = ctx.enter_context(nc.psum_tensor("ps_x", [P, NC_, CAP], F32))
        ps_gu = [ctx.enter_context(nc.psum_tensor(f"ps_gu{i}", [P, 2, 512], F32)) for i in range(2)]
        ps_y = ctx.enter_context(nc.psum_tensor("ps_y", [P, RT, D], F32))

        e_const = sem("e_const")
        settled = sem("e_settled")
        slots_loaded = sem("slots_loaded")
        gu_loaded = [sem(f"gu_loaded{i}") for i in range(2)]
        dn_loaded = [sem(f"dn_loaded{i}") for i in range(2)]
        gathered = [sem(f"gathered{i}") for i in range(4)]
        scattered = sem("scattered")
        added = sem("added")
        idx_ready = sem("idx_ready")
        gu_hi_done = sem("gu_hi_done")
        gu_lo_done = sem("gu_lo_done")
        dn_hi_done = sem("dn_hi_done")
        dn_lo_done = sem("dn_lo_done")
        x_turned = sem("x_turned")
        x_hi_done = sem("x_hi_done")
        x_lo_done = sem("x_lo_done")
        gu_done = sem("gu_done")
        silu_done = sem("silu_done")
        h_done = sem("h_done")
        h_hi_done = sem("h_hi_done")
        h_lo_done = sem("h_lo_done")
        y_filled = sem("y_filled")
        y_read = sem("y_read")

        block = ctx.enter_context(nc.Block())

        def quads(eng, step):
            with eng.Fori(0, E // QUAD - 1) as q:
                for u in range(QUAD):
                    step(q, u, False)
            for u in range(QUAD):
                step(E // QUAD - 1, u, True)

        def count(q, u, ring=1):
            return q * (QUAD // ring) + (u // ring + 1)

        def settle(eng):
            eng.sem_inc(settled, 1)

        @block.sync
        def _(sp):
            sp.dma_start(slots[:, :], table.rearrange("(p n) a -> p (n a)", p=P)).then_inc(slots_loaded, 16)
            sp.wait_ge(e_const, 2)
            with sp.Fori(0, E // QUAD) as q:
                for u in range(QUAD):
                    e = q * QUAD + u
                    i = u % 2
                    sp.wait_ge(gu_lo_done, count(q, u))
                    sp.dma_start(gu[i][:, :, :], gate_up[bass.ds(e, 1), :, :].rearrange("a (p c) n -> (a p) c n", c=NC_)).then_inc(gu_loaded[i], 16)
                    sp.wait_ge(dn_lo_done, count(q, u))
                    sp.dma_start(dn[i][:, 0, :], down[bass.ds(e, 1), 0:P, :].rearrange("a p n -> (a p) n")).then_inc(dn_loaded[i], 16)
                    sp.dma_start(dn[i][P - MIX:P, 1, :], down[bass.ds(e, 1), P:I, :].rearrange("a p n -> (a p) n")).then_inc(dn_loaded[i], 16)

        @block.gpsimd
        def _(pool):
            pool.memset(ident[:, :], 0.0)
            for i in range(2):
                pool.memset(dn[i][:, 1, :], 0.0)
                last = pool.memset(h[i][:, 1, :], 0.0)
            last.then_inc(e_const, 1)
            pool.wait_ge(e_const, 1)
            pool.affine_select(out=ident[:, :], in_=ident[:, :], compare_op=ALU.not_equal, fill=1.0,
                               base=0, pattern=[[-1, P]], channel_multiplier=1).then_inc(e_const, 1)

            def gather(q, u):
                i = u % 4
                e = q * QUAD + u
                settle(pool)
                pool.tensor_copy(idx[i][:, :], slots[:, bass.ds(e * RT, RT)]).then_inc(idx_ready, 1)
                pool.wait_ge(idx_ready, count(q, u))
                settle(pool)
                for t in range(RT):
                    pool.indirect_dma_start(xe[i][:, t, :], None, xg,
                                            bass.IndirectOffsetOnAxis(ap=idx[i][:, t:t + 1], axis=0)).then_inc(gathered[i], 16)

            def step(q, u, last):
                if not (last and u + 3 >= QUAD):
                    pool.wait_ge(y_read, q * QUAD + (u + 2))
                    gather(q, u + 3)
                pool.wait_ge(y_read, q * QUAD + (u + 3))
                settle(pool)
                for t in range(RT):
                    pool.indirect_dma_start(acc, bass.IndirectOffsetOnAxis(ap=idx[u % 4][:, t:t + 1], axis=0),
                                            y[u % 2][:, t, :], None, compute_op=ALU.add).then_inc(scattered, 16)
                pool.wait_ge(scattered, (q * QUAD + (u + 1)) * (16 * RT))
                pool.sem_inc(added, 1)

            pool.wait_ge(slots_loaded, 16)
            for u in range(3):
                gather(0, u)
            quads(pool, step)

        @block.tensor
        def _(pe):
            def turn(q, u):
                pe.wait_ge(gathered[u % 4], (q + (u // 4 + 1)) * (16 * RT))
                pe.wait_ge(x_lo_done, q * QUAD + (u + 1))
                for t in range(RT):
                    for c in range(NC_):
                        last = nc.tensor.transpose(ps_x[:, c, t * P:(t + 1) * P], xe[u % 4][:, t, c:D:NC_], ident[:, :])
                last.then_inc(x_turned, 1)

            def three_passes(dst, pairs):
                ops = [(s, m) for s_hi, s_lo, m_hi, m_lo in pairs for s, m in ((s_hi, m_hi), (s_hi, m_lo), (s_lo, m_hi))]
                for n, (s, m) in enumerate(ops):
                    last = nc.tensor.matmul(dst, s, m, start=(n == 0), stop=(n == len(ops) - 1))
                return last

            def inner(q, u):
                i = u % 2
                pe.wait_ge(gu_lo_done, q * QUAD + (u + 1 + 2))
                pe.wait_ge(x_lo_done, q * QUAD + (u + 1 + 1))
                pe.wait_ge(h_done, q * QUAD + (u - 1 + 2))
                dsts = (ps_gu[i][:, 0, 0:CAP], ps_gu[i][:, 0, CAP:2 * CAP], ps_gu[i][:, 1, 0:CAP])
                for m, dst in enumerate(dsts):
                    cols = slice(m * P, (m + 1) * P)
                    last = three_passes(dst, [(gu_hi[i][:, c, cols], gu_lo[i][:, c, cols], xT_hi[i][:, c, :], xT_lo[i][:, c, :])
                                              for c in range(NC_)])
                last.then_inc(gu_done, 1)

            def outer(q, u):
                i = u % 2
                pe.wait_ge(dn_lo_done, q * QUAD + (u + 1 + 2))
                pe.wait_ge(h_lo_done, q * QUAD + (u + 1))
                pe.wait_ge(y_read, q * QUAD + (u + 2))
                for t in range(RT):
                    rows = slice(t * P, (t + 1) * P)
                    last = three_passes(ps_y[:, t, :], [(h_hi[i][:, k, rows], h_lo[i][:, k, rows], dn_hi[i][:, k, :], dn_lo[i][:, k, :])
                                                        for k in range(2)])
                last.then_inc(y_filled, 1)

            def step(q, u, last):
                if not (last and u + 1 >= QUAD):
                    inner(q, u + 1)
                if not (last and u + 2 >= QUAD):
                    turn(q, u + 2)
                outer(q, u)

            pe.sem_inc(gu_done, 2)
            pe.wait_ge(e_const, 2)
            turn(0, 0)
            turn(0, 1)
            inner(0, 0)
            quads(pe, step)

        @block.scalar
        def _(act):
            def high_gu(q, u):
                i = u % 2
                act.wait_ge(gu_loaded[i], (q * 2 + (u // 2 + 1)) * 16)
                act.wait_ge(gu_done, q * QUAD + (u - 1 + 2))
                act.activation(gu_hi[i][:, :, :], gu[i][:, :, :], ACT.Copy).then_inc(gu_hi_done, 1)

            def high_dn(q, u):
                i = u % 2
                act.wait_ge(dn_loaded[i], (q * 2 + (u // 2 + 1)) * 32)
                act.wait_ge(y_filled, q * QUAD + (u - 1 + 2))
                act.activation(dn_hi[i][:, :, :], dn[i][:, :, :], ACT.Copy).then_inc(dn_hi_done, 1)

            def high_x(q, u):
                act.wait_ge(x_turned, q * QUAD + (u + 1))
                act.wait_ge(gu_done, q * QUAD + (u - 1 + 2))
                act.activation(xT_hi[u % 2][:, :, :], ps_x[:, :, :], ACT.Copy).then_inc(x_hi_done, 1)

            def gate(q, u):
                i = u % 2
                act.wait_ge(gu_done, q * QUAD + (u + 1 + 2))
                act.wait_ge(h_done, q * QUAD + (u - 1 + 2))
                act.activation(silu[i][:, 0, :], ps_gu[i][:, 0, 0:CAP], ACT.Silu)
                act.activation(silu[i][P - MIX:P, 1, :], ps_gu[i][0:MIX, 1, 0:CAP], ACT.Silu).then_inc(silu_done, 1)

            def high_h(q, u):
                i = u % 2
                act.wait_ge(h_done, q * QUAD + (u + 1 + 2))
                act.wait_ge(y_filled, q * QUAD + (u - 1 + 2))
                act.activation(h_hi[i][:, :, :], h[i][:, :, :], ACT.Copy).then_inc(h_hi_done, 1)

            def weigh(q, u):
                i = u % 2
                e = q * QUAD + u
                act.wait_ge(y_filled, q * QUAD + (u + 1 + 2))
                act.wait_ge(added, q * QUAD + (u - 1 + 2))
                settle(act)
                for t in range(RT):
                    last = act.activation(y[i][:, t, :], ps_y[:, t, :], ACT.Identity, scale=xe[u % 4][:, t, bass.ds(D + e, 1)])
                last.then_inc(y_read, 1)

            def step(q, u, last):
                if not (last and u + 1 >= QUAD):
                    high_dn(q, u + 1)
                    gate(q, u + 1)
                if not (last and u + 2 >= QUAD):
                    high_gu(q, u + 2)
                    high_x(q, u + 2)
                if not (last and u + 1 >= QUAD):
                    high_h(q, u + 1)
                weigh(q, u)

            act.sem_inc(y_filled, 2)
            act.sem_inc(added, 2)
            act.sem_inc(y_read, 2)
            act.wait_ge(e_const, 2)
            high_gu(0, 0)
            high_x(0, 0)
            high_dn(0, 0)
            high_gu(0, 1)
            high_x(0, 1)
            gate(0, 0)
            high_h(0, 0)
            quads(act, step)

        @block.vector
        def _(dve):
            def low_gu(q, u):
                i = u % 2
                dve.wait_ge(gu_hi_done, q * QUAD + (u + 1))
                dve.tensor_tensor(gu_lo[i][:, :, :], gu[i][:, :, :], gu_hi[i][:, :, :], ALU.subtract).then_inc(gu_lo_done, 1)

            def low_dn(q, u):
                i = u % 2
                dve.wait_ge(dn_hi_done, q * QUAD + (u + 1))
                dve.tensor_tensor(dn_lo[i][:, :, :], dn[i][:, :, :], dn_hi[i][:, :, :], ALU.subtract).then_inc(dn_lo_done, 1)

            def low_x(q, u):
                dve.wait_ge(x_hi_done, q * QUAD + (u + 1))
                dve.tensor_tensor(xT_lo[u % 2][:, :, :], ps_x[:, :, :], xT_hi[u % 2][:, :, :], ALU.subtract).then_inc(x_lo_done, 1)

            def product(q, u):
                i = u % 2
                dve.wait_ge(silu_done, q * QUAD + (u + 1))
                dve.tensor_tensor(h[i][:, 0, :], silu[i][:, 0, :], ps_gu[i][:, 0, CAP:2 * CAP], ALU.mult)
                dve.tensor_tensor(h[i][P - MIX:P, 1, :], silu[i][P - MIX:P, 1, :], ps_gu[i][P - MIX:P, 1, 0:CAP],
                                  ALU.mult).then_inc(h_done, 1)

            def low_h(q, u):
                i = u % 2
                dve.wait_ge(h_hi_done, q * QUAD + (u + 1))
                dve.tensor_tensor(h_lo[i][:, :, :], h[i][:, :, :], h_hi[i][:, :, :], ALU.subtract).then_inc(h_lo_done, 1)

            def step(q, u, last):
                if not (last and u + 1 >= QUAD):
                    low_dn(q, u + 1)
                    product(q, u + 1)
                if not (last and u + 2 >= QUAD):
                    low_gu(q, u + 2)
                    low_x(q, u + 2)
                if not (last and u + 1 >= QUAD):
                    low_h(q, u + 1)

            dve.sem_inc(gu_lo_done, 2)
            dve.sem_inc(dn_lo_done, 2)
            dve.sem_inc(h_done, 2)
            dve.sem_inc(x_lo_done, 1)
            low_gu(0, 0)
            low_x(0, 0)
            low_dn(0, 0)
            low_gu(0, 1)
            low_x(0, 1)
            product(0, 0)
            low_h(0, 0)
            quads(dve, step)


def final_phase(nc, acc, out):
    with ExitStack() as ctx:
        def sb(name, shape, dt=F32):
            return ctx.enter_context(nc.sbuf_tensor(name, shape, dt))

        def sem(name):
            return ctx.enter_context(nc.semaphore(name))

        r = [sb(f"r{b}", [P, NT, D]) for b in range(B)]
        stats = sb("fstats", [P, B, NT, 6])
        mv = sb("fmv", [P, B, NT, 2])
        var = sb("fvar", [P, B, NT])
        rstd = sb("frstd", [P, B, NT])
        power = sb("fpower", [P, NT])
        loaded = [sem(f"loaded{b}") for b in range(B)]
        f_const = sem("f_const")
        f_moments = sem("f_moments")
        f_var = sem("f_var")
        f_rstd = sem("f_rstd")
        f_normed = sem("f_normed")
        stored = sem("stored")
        block = ctx.enter_context(nc.Block())

        @block.sync
        def _(sp):
            for b in range(B):
                sp.dma_start(r[b][:, :, :], acc[b * S:(b + 1) * S, :].rearrange("(t p) d -> p t d", p=P)).then_inc(loaded[b], 16)
            for b in range(B):
                sp.wait_ge(f_normed, b + 1)
                sp.dma_start(out[b].rearrange("(t p) d -> p t d", p=P), r[b][:, :, :]).then_inc(stored, 16)
            sp.wait_ge(stored, 16 * B)

        @block.gpsimd
        def _(pool):
            pool.memset(power[:, :], -0.5).then_inc(f_const, 1)
            for b in range(B):
                pool.wait_ge(f_moments, b + 1)
                pool.tensor_scalar(var[:, b, :], mv[:, b, :, 1], EPS, 0.0, ALU.add, ALU.add).then_inc(f_var, 1)
                pool.wait_ge(f_const, 1)
                pool.wait_ge(f_var, b + 1)
                pool.tensor_tensor(rstd[:, b, :], var[:, b, :], power[:, :], ALU.pow).then_inc(f_rstd, 1)

        @block.vector
        def _(dve):
            def moments(b):
                dve.wait_ge(loaded[b], 16)
                for t in range(NT):
                    dve.bn_stats(stats[:, b, t, :], r[b][:, t, :])
                dve.drain()
                for t in range(NT):
                    last = dve.bn_aggr(mv[:, b, t, :], stats[:, b, t, :])
                last.then_inc(f_moments, 1)

            moments(0)
            for b in range(B):
                if b + 1 < B:
                    moments(b + 1)
                dve.wait_ge(f_rstd, b + 1)
                for t in range(NT):
                    last = dve.tensor_scalar(r[b][:, t, :], r[b][:, t, :], mv[:, b, t, 0:1], rstd[:, b, t:t + 1],
                                             ALU.subtract, ALU.mult)
                last.then_inc(f_normed, 1)


_INS = ['x', 'ctx_2048', 'L0_attn_ln_g', 'L0_attn_ln_b', 'L0_attn_Wq', 'L0_attn_bq', 'L0_attn_Wk', 'L0_attn_bk',
        'L0_attn_Wv', 'L0_attn_bv', 'L0_attn_Wo', 'L0_attn_bo', 'L0_ffn_router_weight']


def kernel(**inputs):
    import numpy as _np
    import concourse.bacc as _bacc
    from concourse import mybir as _mybir
    from concourse.bass_utils import run_bass_kernel_spmd as _run

    given = {n: _np.ascontiguousarray(inputs[n]) for n in _INS}
    gate, up = _np.asarray(inputs['L0_ffn_gate_proj']), _np.asarray(inputs['L0_ffn_up_proj'])
    given['gate_up'] = _np.concatenate([gate[:, :, :P], up[:, :, :P], gate[:, :, P:], up[:, :, P:]], axis=2)
    given['down'] = _np.ascontiguousarray(inputs['L0_ffn_down_proj'])

    nc = _bacc.Bacc("TRN2", target_bir_lowering=False, num_devices=1)
    arrays, args = {}, []
    for name, a in given.items():
        arrays[f"in_{name}"] = a
        args.append(nc.dram_tensor(f"in_{name}", a.shape, _mybir.dt.from_np(a.dtype), kind="ExternalInput").ap())
    args.append(nc.dram_tensor("out_x", (B, S, D), F32, kind="ExternalOutput").ap())
    kernel_body(nc, *args)
    r = _run(nc, [arrays], core_ids=[0])
    return r.results[0]["out_x"]
```

```python
from contextlib import ExitStack

import concourse.bass as bass
from concourse import mybir

F32 = mybir.dt.float32
F32R = mybir.dt.float32r
BF16 = mybir.dt.bfloat16
I32 = mybir.dt.int32
ALU = mybir.AluOpType
ACT = mybir.ActivationFunctionType
AX = mybir.AxisListType

P = 128
B, S, D = 4, 512, 512
H, DH = 16, 32
NC_ = D // P
NT = S // P
HG = P // DH
E, I, TOPK = 64, 192, 8
CAP = 2 * (2 * 512 * TOPK) // E
TOK = B * S
SLOTS = E * CAP
XROW = D + E
EPS = 1e-5
SCALE = float(DH) ** -0.5
MASKED = -1.0e30
MASKED_BIAS = 10000.0
BIG = 3.0e38
HEADS = NC_ * NT * HG
UNITS = NC_ * NT
LOOK = 2
PROBS = 4
TURNED = 8
PRIME = 64


def attention_steps(a):
    per_group = NT * HG
    for i in range(HEADS + LOOK + 3):
        if i < HEADS:
            yield ("scores", a, i)
        n = i - LOOK
        if 0 <= n < HEADS:
            yield ("probsT", a, n)
        if i < HEADS and a == 1 and i % per_group == per_group - 1:
            yield ("masked", a, i // per_group)
        n -= 1
        if 0 <= n < HEADS and n % HG == HG - 1:
            unit = n // HG
            yield ("values", a, unit)
            if unit % NT == NT - 1:
                yield ("outcopy", a, unit // NT)
            if a == 1 and unit == UNITS - 1:
                yield ("norm0", 0, 0)
        n -= 1
        if 0 <= n < HEADS and n % per_group == per_group - 1:
            yield ("outT", a, n // per_group)
            yield ("normalize", a, n // per_group)
        g = i // per_group
        if i % per_group == 0 and (a, g) in [(0, 0), (0, 1), (0, 2), (0, 3), (1, 1), (1, 2)]:
            yield ("k", a, g + 1) if g + 1 < NC_ else ("k", 1, 0)
        if i % per_group == 3 and g + 1 < NC_:
            yield ("q", a, g + 1)
        if g == NC_ - 1 and i % per_group in (8, 10, 12) and a == 0:
            yield ("oT", 0, (i % per_group - 8) // 2)
        if g == NC_ - 1 and i % per_group in (2, 5, 8, 11) and a == 1:
            yield ("moments0", 0, i % per_group // 3)


def batch_steps():
    yield from attention_steps(0)
    yield ("projA", 0, 0)
    yield ("oT", 0, NC_ - 1)
    yield from (("proj", 0, t) for t in range(NT))
    yield from (("suffix", 1, t) for t in range(2))
    yield ("norm1", 0, 0)
    yield ("q", 1, 0)
    yield ("k", 1, 1)
    yield from (("suffix", 1, t) for t in range(2, NT))
    yield from attention_steps(1)
    yield from (("xT", 0, c) for c in range(2))
    yield ("residual", 1, 0)
    yield from (("xT", 0, c) for c in range(2, NC_))
    yield ("k", 0, 0)
    yield ("norm2", 1, 0)
    yield ("q", 0, 0)
    yield from (("x2T", 1, t) for t in range(NT))
    yield ("logits", 1, 0)
    yield ("v", 0, 0)
    yield ("places", 1, 0)
    yield from (("v", 0, t) for t in range(1, NT))


STEPS = list(batch_steps())
AHEAD = [s for s in STEPS if s[0] in ("moments0", "norm0", "xT", "v") or s in (("k", 0, 0), ("q", 0, 0))]
AHEAD_BANK = {s: n for n, s in enumerate(s for s in AHEAD if s[0] in "xTkqv")}
RING = 3
USERS = [s for s in STEPS if s not in AHEAD and s[0] in
         ("q", "k", "probsT", "outT", "oT", "suffix", "x2T", "logits", "places")]
RING_USE = {s: n for n, s in enumerate(USERS)}
PER_BANK = [len([n for n in range(len(USERS)) if n % RING == r]) for r in range(RING)]


def copies_first(steps):
    steps = list(steps)
    for s in [s for s in steps if s[0] == "scores" and s[2] >= LOOK]:
        steps.remove(s)
        steps.insert(steps.index(("probsT", s[1], s[2] - LOOK)) + 1, s)
    return steps


def whole_program(eng, do, steps=STEPS):
    for step in AHEAD:
        do(0, step)
    with eng.Fori(0, B - 1) as b:
        for step in steps:
            do(b + 1 if step in AHEAD else b, step)
    for step in steps:
        if step not in AHEAD:
            do(B - 1, step)


MADE = {s: n for n, s in enumerate([s for s in AHEAD if s[0] in "kq"] + [s for s in STEPS if s[0] in ("k", "q") and s not in AHEAD])}
STACK_INC = 16 * 3 * HG
SHARE_INC = 16 * HG
SHARED = {w: [NC_ - 1, NC_ + 1, NC_ + 2, NC_ + 3] for w in "kq"}
LATE = ("q", NC_)


def is_shared(w, u):
    return (w, u) == LATE or u in SHARED[w]


def stack_count(w, u):
    return sum(STACK_INC - (SHARE_INC if v in SHARED[w] else 0) for v in range(u % 2, u + 1, 2) if (w, v) != LATE)


def kernel_body(nc, x, ctx_in, ln_g, ln_b, Wq, bq, Wk, bk, Wv, bv, Wo, bo, Wr, gate_up, down, out):
    xg = nc.dram_tensor("x2_and_gates", [TOK + CAP, XROW], F32).ap()
    acc = nc.dram_tensor("residual_sum", [TOK + CAP, D], F32).ap()
    table = nc.dram_tensor("slot_token", [SLOTS, 1], I32).ap()
    attention_phase(nc, x, ctx_in, ln_g, ln_b, Wq, bq, Wk, bk, Wv, bv, Wo, bo, Wr, xg, acc, table)
    expert_phase(nc, gate_up, down, xg, acc, table)
    final_phase(nc, acc, out)


def attention_phase(nc, x, ctx_in, ln_g, ln_b, Wq, bq, Wk, bk, Wv, bv, Wo, bo, Wr, xg, acc, table):
    with ExitStack() as ctx:
        def sb(name, shape, dt=F32):
            return ctx.enter_context(nc.sbuf_tensor(name, shape, dt))

        def sem(name):
            return ctx.enter_context(nc.semaphore(name))

        xin = sb("xin", [P, NT, D])
        ctxv = sb("ctxv", [P, NT, D])
        x1 = sb("x1", [P, NT, D])
        o_sb = sb("o_sb", [P, NT, D])
        vals = sb("vals", [P, NT, D])
        suffix = vals
        xT_hi = sb("xT_hi", [P, NC_, S], F32R)
        xT_lo = sb("xT_lo", [P, NC_, S], F32R)
        w_hi = [sb(f"w_hi{i}", [P, NC_, D], F32R) for i in range(4)]
        w_lo = [sb(f"w_lo{i}", [P, NC_, D], F32R) for i in range(4)]
        staging, PART = (x1, vals, o_sb, x1), (1, 0, 2, 3)
        part = {(w, p): sb(f"part_{w}_{p}", [P, S], F32R) for w in "qk" for p in ("hi", "lo")}
        stack = {(w, i): sb(f"stack_{w}{i}", [3 * DH, HG, S], F32R) for w in "qk" for i in range(2)}
        v_tmp = sb("v_tmp", [P, S])
        probs = [sb(f"probs{i}", [P, S]) for i in range(PROBS)]
        probsT = [sb(f"probsT{i}", [P, S]) for i in range(TURNED)]
        outT = sb("outT", [P, S])
        scaled = (v_tmp, outT)
        mask = sb("mask", [P, S])
        neg_max = [sb(f"neg_max{i}", [P, NT, HG]) for i in range(2)]
        denom = [sb(f"denom{i}", [P, NT, HG]) for i in range(2)]
        rdenom = sb("rdenom", [P, NT, HG])
        e_mask = sb("e_mask", [P, NT, HG])
        e_cnt = sb("e_cnt", [P, NT, HG])
        tail = sb("tail", [P, NT, P])
        behind = sb("behind", [P, NT])
        least = sb("least", [P, 2])
        ident = sb("ident", [P, P])
        tri = sb("tri", [P, P])
        ones = sb("ones", [P, P])
        tri_before = sb("tri_before", [P, P], BF16)
        ones_bf = sb("ones_bf", [P, P], BF16)
        gcol = sb("gcol", [P, NC_])
        bcol = sb("bcol", [P, NC_])
        bqcol = sb("bqcol", [P, NC_])
        bkcol = sb("bkcol", [P, NC_])
        bv_rows = sb("bv_rows", [P, D])
        bo_rows = sb("bo_rows", [P, D])
        wr_sb = sb("wr_sb", [P, NC_, E])
        minus_bias = sb("minus_bias", [P, 1])
        stats = [sb(f"stats{i}", [P, NT, 6]) for i in range(2)]
        mv = [sb(f"mv{i}", [P, NT, 2]) for i in range(2)]
        var = [sb(f"var{i}", [P, NT]) for i in range(2)]
        rstd = [sb(f"rstd{i}", [P, NT]) for i in range(2)]
        power = sb("power", [P, NT])
        logit = sb("logit", [P, NT, E])
        left = sb("left", [P, NT, E])
        chosen = sb("chosen", [P, NT, E])
        chosen_bf = sb("chosen_bf", [P, NT, E], BF16)
        chosen_sum = sb("chosen_sum", [P, E], BF16)
        gates = sb("gates", [P, NT, E])
        top = sb("top", [P, NT, TOPK])
        neg_top = sb("neg_top", [P, NT])
        gsum = sb("gsum", [P, NT])
        rgsum = sb("rgsum", [P, NT])
        place, wrap = logit, left
        col2e = sb("col2e", [P, NT, E])
        key8 = sb("key8", [P, NT, TOPK])
        gone8 = sb("gone8", [P, NT, TOPK])
        slot8 = sb("slot8", [P, NT, TOPK], I32)
        ids_all = sb("ids_all", [P, B, NT], I32)
        ids = sb("ids", [P, NT], I32)
        pad_ids = sb("pad_ids", [P, P], I32)

        s_bank = [ctx.enter_context(nc.psum_tensor(f"s_bank{i}", [P, 512], F32)) for i in range(4)]
        ring = [ctx.enter_context(nc.psum_tensor(f"ring{i}", [P, 512], F32)) for i in range(RING)]
        o_bank = ctx.enter_context(nc.psum_tensor("o_bank", [P, S], F32))

        cols_loaded = sem("cols_loaded")
        consts_loaded = sem("consts_loaded")
        w_loaded = [sem(f"w_loaded{i}") for i in range(4)]
        w_high = sem("w_high")
        pool_ready = sem("pool_ready")
        dve_ready = sem("dve_ready")
        x_loaded = sem("x_loaded")
        ctx_loaded = sem("ctx_loaded")
        x_used = sem("x_used")
        ahead_filled = sem("ahead_filled")
        ahead_freed = sem("ahead_freed")
        v_ready = sem("v_ready")
        projected = sem("projected")
        filled = sem("filled")
        freed = [sem(f"freed{r}") for r in range(RING)]
        scored = sem("scored")
        maxed = sem("maxed")
        exped = sem("exped")
        pv_done = sem("pv_done")
        o_copied = sem("o_copied")
        o_normed = sem("o_normed")
        part_hi = sem("part_hi")
        xt_hi = sem("xt_hi")
        xt_ready = sem("xt_ready")
        stacked = {(w, i): sem(f"stacked_{w}{i}") for w in "kq" for i in range(2)}
        late_high = [sem(f"late_high{j}") for j in range(HG)]
        late_low = [sem(f"late_low{j}") for j in range(HG)]
        shared_stacked = {w: sem(f"shared_stacked_{w}") for w in "kq"}
        e_ready = sem("e_ready")
        tail_ready = sem("tail_ready")
        tail_step = sem("tail_step")
        o_raw = sem("o_raw")
        divided = sem("divided")
        resid_done = sem("resid_done")
        settled = sem("settled")
        stat_ready = [sem(f"stat_ready{i}") for i in range(2)]
        rstd_step = [sem(f"rstd_step{i}") for i in range(2)]
        rstd_ready = [sem(f"rstd_ready{i}") for i in range(2)]
        normed = [sem(f"normed{i}") for i in range(2)]
        res_ready = sem("res_ready")
        logits_ready = sem("logits_ready")
        gexp_ready = sem("gexp_ready")
        chosen_ready = sem("chosen_ready")
        routed = sem("routed")
        ids_ready = sem("ids_ready")
        x2_stored = sem("x2_stored")
        tokens_stored = sem("tokens_stored")
        gates_stored = sem("gates_stored")
        slots_free = sem("slots_free")
        init_stored = sem("init_stored")

        INIT_STORES = 16 * (1 + 4 * (CAP // P))

        def ring_use(step):
            n = RING_USE[step]
            return n, n % RING, n // RING

        def last_uses(steps):
            uses = [ring_use(step)[1:] for step in steps]
            return [(r, max(k for s, k in uses if s == r)) for r in sorted({r for r, _ in uses})]

        def wait_filled(eng, b, step):
            if step in AHEAD_BANK:
                eng.wait_ge(ahead_filled, b * len(AHEAD_BANK) + (AHEAD_BANK[step] + 1))
                return
            eng.wait_ge(filled, b * len(USERS) + (RING_USE[step] + 1))

        def bank_of(step):
            if step in AHEAD_BANK:
                return s_bank[AHEAD_BANK[step] % 4]
            return ring[ring_use(step)[1]] if step in RING_USE else None

        def freed_by(step):
            if step in AHEAD_BANK:
                return v_ready if step[0] == "v" else ahead_freed
            return freed[ring_use(step)[1]] if step in RING_USE else None

        def wait_freed(eng, b, step):
            if step[0] == "v":
                eng.wait_ge(v_ready, b * NT + (step[2] + 1))
            elif step in AHEAD_BANK:
                eng.wait_ge(ahead_freed, b * 2 + (1 if step[0] == "k" else 2))
            else:
                _, r, k = ring_use(step)
                eng.wait_ge(freed[r], b * PER_BANK[r] + (k + 1 + PRIME))

        def tiles_of(src, b):
            return src[bass.ds(b, 1), :, :].rearrange("a (t p) d -> (a p) t d", p=P)

        def settle(eng):
            eng.sem_inc(settled, 1)

        def first_batch(b):
            return isinstance(b, int) and b == 0

        def wait_stacked(eng, b, w, u):
            if (w, u) == LATE:
                return
            eng.wait_ge(stacked[w, u % 2], b * stack_count(w, 2 * NC_ - 2 + u % 2) + (stack_count(w, u) + PRIME))
            if u in SHARED[w]:
                eng.wait_ge(shared_stacked[w], b * (SHARE_INC * len(SHARED[w])) + SHARE_INC * (SHARED[w].index(u) + 1))

        def stack_use(a, g):
            u = a * NC_ + g
            return u % 2, u // 2

        block = ctx.enter_context(nc.Block())

        @block.sync
        def _(sp):
            sp.dma_start(xin[:, :, :], tiles_of(x, 0)).then_inc(x_loaded, 16)
            with nc.allow_non_contiguous_dma(reason="a few vectors laid along partitions"):
                for vec, col in ((ln_g, gcol), (ln_b, bcol), (bq, bqcol), (bk, bkcol)):
                    sp.dma_start(col[:, :], vec.rearrange("(c p) -> p c", p=P)).then_inc(cols_loaded, 16)
            def load_weights(i):
                w = (Wk, Wq, Wv, Wo)[i]
                sp.dma_start(staging[i][:, :, :], w.rearrange("(c p) n -> p c n", p=P)).then_inc(w_loaded[i], 16)

            for i in range(3):
                load_weights(i)
            sp.dma_start(bv_rows[:, :], bv.rearrange("(a n) -> a n", a=1).to_broadcast([P, D])).then_inc(consts_loaded, 16)
            sp.dma_start(bo_rows[:, :], bo.rearrange("(a n) -> a n", a=1).to_broadcast([P, D])).then_inc(consts_loaded, 16)
            sp.dma_start(wr_sb[:, :, :], Wr.rearrange("(c p) e -> p c e", p=P)).then_inc(consts_loaded, 16)
            sp.wait_ge(pool_ready, 2)
            sp.dma_start(table.rearrange("(p n) a -> p (n a)", p=P), pad_ids[:, :]).then_inc(init_stored, 16)
            for h in range(CAP // P):
                rows = slice(TOK + h * P, TOK + (h + 1) * P)
                for dst, width in ((xg, XROW), (acc, D)):
                    sp.dma_start(dst[rows, 0:S - P], mask[:, 0:S - P]).then_inc(init_stored, 16)
                    sp.dma_start(dst[rows, S - P:width], mask[:, 0:width - (S - P)]).then_inc(init_stored, 16)

            sp.wait_ge(dve_ready, 1)
            load_weights(3)

            def load_x(b):
                sp.wait_ge(x_used, b + 1)
                sp.dma_start(xin[:, :, :], tiles_of(x, b)).then_inc(x_loaded, 16)

            def load_context(b):
                sp.wait_ge(ahead_filled, b * len(AHEAD_BANK) + NC_)
                settle(sp)
                sp.dma_start(ctxv[:, :, :], tiles_of(ctx_in, b)).then_inc(ctx_loaded, 16)

            def stack_group(b, a, g, which="kq"):
                buf, n = stack_use(a, g)
                sp.wait_ge(scored, b * (2 * HEADS) + ((a * NC_ + g - 1) * NT * HG + PRIME))
                settle(sp)
                for w in which:
                    order = ("hi", "lo", "hi") if w == "k" else ("hi", "hi", "lo")
                    if (w, a * NC_ + g) == LATE:
                        sp.wait_ge(part_hi, b * (4 * NC_) + (MADE[w, a, g] + 1))
                        settle(sp)
                        for j in range(HG):
                            for q in range(2):
                                sp.dma_start(stack[w, buf][DH * q:DH * (q + 1), j, :].bitcast(F32),
                                             part[w, "hi"][DH * j:DH * (j + 1), :].bitcast(F32)).then_inc(late_high[j], 16)
                        continue
                    wait_freed(sp, b, (w, a, g))
                    settle(sp)
                    for q, p in enumerate(order):
                        if q == 2 and is_shared(w, a * NC_ + g):
                            continue
                        for j in range(HG):
                            sp.dma_start(stack[w, buf][DH * q:DH * (q + 1), j, :].bitcast(F32),
                                         part[w, p][DH * j:DH * (j + 1), :].bitcast(F32)).then_inc(stacked[w, buf], 16)

            def batch(b, last):
                for g in range(1, NC_):
                    stack_group(b, 0, g)
                stack_group(b, 1, 0, "k")
                stack_group(b, 1, 0, "q")
                stack_group(b, 1, 1, "k")
                stack_group(b, 1, 1, "q")
                if not last:
                    load_x(b + 1)
                for g in range(2, NC_):
                    stack_group(b, 1, g)
                if not last:
                    load_context(b + 1)
                    stack_group(b + 1, 0, 0)
                sp.wait_ge(normed[1], b * 2 + 2)
                settle(sp)
                for dst in (xg[bass.ds(b * S, S), 0:D], acc[bass.ds(b * S, S), :]):
                    sp.dma_start(dst.rearrange("(t p) d -> p t d", p=P), o_sb[:, :, :]).then_inc(x2_stored, 16)

            load_context(0)
            stack_group(0, 0, 0)
            with sp.Fori(0, B - 1) as b:
                batch(b, last=False)
            batch(B - 1, last=True)
            sp.wait_ge(x2_stored, B * 32 + PRIME)
            sp.wait_ge(init_stored, INIT_STORES)

        @block.gpsimd
        def _(pool):
            pool.iota(pad_ids[:, :], [[0, E], [P, 2]], base=TOK, channel_multiplier=1).then_inc(pool_ready, 1)
            for buf, v in ((ident, 0.0), (tri, 1.0), (ones, 1.0), (mask, 0.0), (tri_before, 1.0),
                           (ones_bf, 1.0), (power, -0.5), (minus_bias, -MASKED_BIAS), (chosen_sum, 0.0)):
                pool.memset(buf[:, :], v)
            pool.memset(least[:, :], MASKED_BIAS)
            pool.iota(ids_all[:, :, :], [[S, B], [P, NT]], base=0, channel_multiplier=1)
            pool.iota(col2e[:, :, :], [[0, NT], [2, E]], base=1, channel_multiplier=0,
                      allow_small_or_imprecise_dtypes=True)
            pool.iota(behind[:, :], [[-P, NT]], base=S - 1, channel_multiplier=-1,
                      allow_small_or_imprecise_dtypes=True).then_inc(pool_ready, 1)
            pool.wait_ge(pool_ready, 2)
            pool.affine_select(out=ident[:, :], in_=ident[:, :], compare_op=ALU.not_equal, fill=1.0,
                               base=0, pattern=[[-1, P]], channel_multiplier=1)
            pool.affine_select(out=tri[:, :], in_=tri[:, :], compare_op=ALU.is_gt, fill=0.0,
                               base=0, pattern=[[-1, P]], channel_multiplier=1)
            pool.affine_select(out=tri_before[:, :], in_=tri_before[:, :], compare_op=ALU.is_gt, fill=0.0,
                               base=0, pattern=[[1, P]], channel_multiplier=-1)
            pool.affine_select(out=mask[:, S - P:S], in_=mask[:, S - P:S], compare_op=ALU.is_ge, fill=MASKED,
                               base=0, pattern=[[-1, P]], channel_multiplier=1)
            pool.affine_select(out=least[:, 1:2], in_=least[:, 1:2], compare_op=ALU.is_gt, fill=BIG,
                               base=P - 1, pattern=[[0, 1]], channel_multiplier=-1).then_inc(pool_ready, 1)
            def inverse_deviation(i, count):
                pool.wait_ge(stat_ready[i], count)
                settle(pool)
                pool.tensor_scalar(var[i][:, :], mv[i][:, :, 1], EPS, 0.0, ALU.add, ALU.add).then_inc(rstd_step[i], 1)
                pool.wait_ge(rstd_step[i], count)
                pool.tensor_tensor(rstd[i][:, :], var[i][:, :], power[:, :], ALU.pow).then_inc(rstd_ready[i], 1)

            def stack_share(b, a, w, g):
                buf, _ = stack_use(a, g)
                pool.wait_ge(scored, b * (2 * HEADS) + ((a * NC_ + g - 1) * NT * HG + PRIME))
                wait_freed(pool, b, (w, a, g))
                settle(pool)
                for j in range(HG):
                    done = late_low[j] if (w, a * NC_ + g) == LATE else shared_stacked[w]
                    pool.dma_start(stack[w, buf][DH * 2:DH * 3, j, :].bitcast(F32),
                                   part[w, "hi" if w == "k" else "lo"][DH * j:DH * (j + 1), :].bitcast(F32)).then_inc(done, 16)

            def by_head(t):
                return t.rearrange("p t (j d) -> p t j d", d=DH)

            def masked_share(b, n):
                pool.wait_ge(e_ready, b * NC_ + (n + 1))
                settle(pool)
                pool.tensor_tensor(e_cnt[:, :, :], e_mask[:, :, :],
                                   behind[:, :].unsqueeze(2).to_broadcast([P, NT, HG]), ALU.mult).then_inc(tail_step, 1)
                pool.tensor_tensor(by_head(tail[:, :, :]), by_head(suffix[:, :, n * P:(n + 1) * P]),
                                   e_mask[:, :, :].unsqueeze(3).to_broadcast([P, NT, HG, DH]), ALU.mult)
                pool.wait_ge(tail_step, b * NC_ + (n + 1))
                pool.tensor_tensor(e_cnt[:, :, :], denom[n % 2][:, :, :], e_cnt[:, :, :], ALU.add).then_inc(tail_ready, 1)

            def divide(b, n):
                dst = o_sb[:, :, n * P:(n + 1) * P]
                pool.wait_ge(o_raw, b * NC_ + (n + 1))
                settle(pool)
                pool.tensor_tensor(by_head(dst), by_head(tail[:, :, :]),
                                   rdenom[:, :, :].unsqueeze(3).to_broadcast([P, NT, HG, DH]), ALU.mult).then_inc(divided, 1)
                pool.wait_ge(divided, b * NC_ + (n + 1))
                pool.tensor_tensor(dst, dst, x1[:, :, n * P:(n + 1) * P], ALU.add).then_inc(resid_done, 1)


            def batch(b, last):
                pool.wait_ge(x_loaded, b * 16 + 16)
                for t in range(NT):
                    add = pool.tensor_tensor(x1[:, t, :], xin[:, t, :], bo_rows[:, :], ALU.add)
                add.then_inc(res_ready, 1)
                stack_share(b, 0, "k", NC_ - 1)
                stack_share(b, 0, "q", NC_ - 1)
                inverse_deviation(1, b * 2 + 1)
                stack_share(b, 1, "q", 0)
                stack_share(b, 1, "k", 1)
                stack_share(b, 1, "q", 1)
                for n in range(NC_):
                    if n == NC_ - 1 and not last:
                        inverse_deviation(0, b + 2)
                    masked_share(b, n)
                    divide(b, n)
                    if n + 2 < NC_:
                        stack_share(b, 1, "k", n + 2)
                        stack_share(b, 1, "q", n + 2)
                inverse_deviation(1, b * 2 + 2)
                pool.wait_ge(init_stored, INIT_STORES)
                pool.wait_ge(routed, b + 1)
                settle(pool)
                pool.dma_start(xg[bass.ds(b * S, S), D:XROW].rearrange("(t p) d -> p t d", p=P), gates[:, :, :]).then_inc(gates_stored, 16)
                pool.tensor_copy(ids[:, :], ids_all[:, bass.ds(b, 1), :].rearrange("p a t -> p (a t)")).then_inc(ids_ready, 1)
                pool.wait_ge(ids_ready, b + 1)
                settle(pool)
                for t in range(NT):
                    for j in range(TOPK):
                        pool.indirect_dma_start(
                            table, bass.IndirectOffsetOnAxis(ap=slot8[:, t, j:j + 1], axis=0), ids[:, t:t + 1], None,
                            bounds_check=SLOTS - 1, oob_is_err=False).then_inc(tokens_stored, 16)
                pool.wait_ge(gates_stored, (b + 1) * 16)
                pool.wait_ge(tokens_stored, (b + 1) * (16 * NT * TOPK))
                pool.sem_inc(slots_free, 1)

            pool.sem_inc(slots_free, 1)
            pool.sem_inc(tail_ready, PRIME)
            inverse_deviation(0, 1)
            pool.wait_ge(consts_loaded, 16 * 3)
            pool.wait_ge(dve_ready, 4)
            with pool.Fori(0, B - 1) as b:
                batch(b, last=False)
            batch(B - 1, last=True)

        @block.tensor
        def _(pe):
            pe.sem_inc(scored, PRIME)
            pe.wait_ge(pool_ready, 3)

            def bank_free(b, step):
                if step in AHEAD_BANK:
                    before = [t for t, m in AHEAD_BANK.items() if m == AHEAD_BANK[step] - 4]
                    if before and before[0][0] != "xT":
                        wait_freed(pe, b, before[0])
                else:
                    _, r, k = ring_use(step)
                    pe.wait_ge(freed[r], b * PER_BANK[r] + (k + PRIME))
                return bank_of(step)

            def count_up(step):
                return ahead_filled if step in AHEAD_BANK else filled

            def three_passes(dst, pairs, first=True, final=True):
                ops = [(s, m) for s_hi, s_lo, m_hi, m_lo in pairs for s, m in ((s_hi, m_hi), (s_hi, m_lo), (s_lo, m_hi))]
                for i, (s, m) in enumerate(ops):
                    last = nc.tensor.matmul(dst, s, m, start=(first and i == 0), stop=(final and i == len(ops) - 1))
                return last

            def project(t, chunks):
                rows = slice(t * P, (t + 1) * P)
                return three_passes(s_bank[t][:, :], [(xT_hi[:, c, rows], xT_lo[:, c, rows], w_hi[3][:, c, :], w_lo[3][:, c, :])
                                                      for c in chunks], first=(0 in chunks), final=(NC_ - 1 in chunks))

            def transposed(b, step, blocks):
                bank = bank_free(b, step)
                for i, src in enumerate(blocks):
                    last = nc.tensor.transpose(bank[:, P * i:P * (i + 1)], src, ident[:, :])
                last.then_inc(count_up(step), 1)

            def do(b, step):
                kind, a, n = step
                if kind == "xT":
                    if n == 0:
                        pe.wait_ge(normed[0], b + 1)
                    transposed(b, step, [ctxv[:, t, n * P:(n + 1) * P] for t in range(NT)])
                elif kind in "qk" and a == 0:
                    bank = bank_free(b, step)
                    w = 0 if kind == "q" else 1
                    if first_batch(b) and n == 0:
                        pe.wait_ge(dve_ready, 1 if kind == "k" else 2)
                    cols = slice(n * P, (n + 1) * P)
                    for c in range(NC_):
                        if n == 0 and kind == "k":
                            pe.wait_ge(xt_ready, b * (2 * NC_) + (c + 1))
                        last = three_passes(bank[:, :], [(w_hi[w][:, c, cols], w_lo[w][:, c, cols], xT_hi[:, c, :], xT_lo[:, c, :])],
                                            first=(c == 0), final=(c == NC_ - 1))
                    last.then_inc(count_up(step), 1)
                elif kind in "qk":
                    if kind == "k" and n == 0:
                        pe.wait_ge(ctx_loaded, b * 16 + 16)
                    if kind == "q" and n == 0:
                        pe.wait_ge(normed[1], b * 2 + 1)
                    src = x1 if kind == "q" else ctxv
                    transposed(b, step, [src[:, t, n * P:(n + 1) * P] for t in range(NT)])
                elif kind == "v":
                    bank = bank_free(b, step)
                    if first_batch(b) and n == 0:
                        pe.wait_ge(dve_ready, 3)
                    rows = slice(n * P, (n + 1) * P)
                    three_passes(bank[:, :], [(xT_hi[:, c, rows], xT_lo[:, c, rows], w_hi[2][:, c, :], w_lo[2][:, c, :])
                                              for c in range(NC_)]).then_inc(count_up(step), 1)
                elif kind == "scores":
                    g, qi, j = n // (NT * HG), n // HG % NT, n % HG
                    buf, k = stack_use(a, g)
                    if a == 0 and n == 0:
                        wait_freed(pe, b, ("v", 0, NT - 1))
                    if qi == 0 and j == 0:
                        for w in "kq":
                            wait_stacked(pe, b, w, a * NC_ + g)
                    if qi == 0 and ("q", a * NC_ + g) == LATE:
                        pe.wait_ge(late_high[j], b * 32 + 32)
                        pe.wait_ge(late_low[j], b * 16 + 16)
                    pe.wait_ge(exped, b * (2 * HEADS) + (a * HEADS + n - 3 + PRIME))
                    cols = P * (qi + 1)
                    nc.tensor.matmul(s_bank[n % 4][:, 0:cols], stack["q", buf][:, j, qi * P:(qi + 1) * P],
                                     stack["k", buf][:, j, 0:cols], start=True, stop=True).then_inc(scored, 1)
                elif kind == "probsT":
                    qi = n // HG % NT
                    pe.wait_ge(exped, b * (2 * HEADS) + (a * HEADS + n + 1 + PRIME))
                    transposed(b, step, [probs[n % PROBS][:, kb * P:(kb + 1) * P] for kb in range(qi + 1)])
                elif kind == "values":
                    g, qi = n // NT, n % NT
                    if qi == 0:
                        pe.wait_ge(o_copied, b * (2 * NC_) + (a * NC_ + g + PRIME))
                    for r, k in last_uses([("probsT", a, n * HG + j) for j in range(HG)]):
                        pe.wait_ge(freed[r], b * PER_BANK[r] + (k + 1 + PRIME))
                    v = vals if a == 0 else ctxv
                    for kb in range(qi + 1):
                        for j in range(HG):
                            h = g * HG + j
                            last = nc.tensor.matmul(o_bank[j * DH:(j + 1) * DH, qi * P:(qi + 1) * P], v[:, kb, h * DH:(h + 1) * DH],
                                                    probsT[(n * HG + j) % TURNED][:, kb * P:(kb + 1) * P],
                                                    start=(kb == 0), stop=(kb == qi), tile_position=(0, j * DH))
                    last.then_inc(pv_done, 1)
                elif kind == "outT":
                    pe.wait_ge(o_copied, b * (2 * NC_) + (a * NC_ + n + 1 + PRIME))
                    transposed(b, step, [outT[:, t * P:(t + 1) * P] for t in range(NT)])
                elif kind == "oT":
                    pe.wait_ge(o_normed, b * NC_ + (n + 1))
                    transposed(b, step, [o_sb[:, t, n * P:(n + 1) * P] for t in range(NT)])
                elif kind == "projA":
                    pe.wait_ge(dve_ready, 4)
                    for c in range(NC_ - 1):
                        pe.wait_ge(xt_ready, b * (2 * NC_) + (NC_ + c + 1))
                        for t in range(NT):
                            project(t, (c,))
                elif kind == "proj":
                    if n == 0:
                        pe.wait_ge(xt_ready, b * (2 * NC_) + 2 * NC_)
                    project(n, (NC_ - 1,)).then_inc(projected, 1)
                elif kind == "suffix":
                    if n == 0:
                        pe.wait_ge(ctx_loaded, b * 16 + 16)
                    bank = bank_free(b, step)
                    for kb in range(n, NT):
                        last = nc.tensor.matmul(bank[:, :], (tri if kb == n else ones)[:, :], ctxv[:, kb, :],
                                                start=(kb == n), stop=(kb == NT - 1))
                    last.then_inc(filled, 1)
                elif kind == "x2T":
                    if n == 0:
                        pe.wait_ge(normed[1], b * 2 + 2)
                    transposed(b, step, [o_sb[:, n, c * P:(c + 1) * P] for c in range(NC_)])
                elif kind == "logits":
                    pe.wait_ge(consts_loaded, 16 * 3)
                    for r, k in last_uses([("x2T", 1, t) for t in range(NT)]):
                        pe.wait_ge(freed[r], b * PER_BANK[r] + (k + 1 + PRIME))
                    bank = bank_free(b, step)
                    for t in range(NT):
                        for c in range(NC_):
                            last = nc.tensor.matmul(bank[:, E * t:E * (t + 1)], suffix[:, t, c * P:(c + 1) * P],
                                                    wr_sb[:, c, :], start=(c == 0), stop=(c == NC_ - 1))
                    last.then_inc(filled, 1)
                elif kind == "places":
                    pe.wait_ge(chosen_ready, b + 1)
                    bank = bank_free(b, step)
                    for t in range(NT):
                        nc.tensor.matmul(bank[:, E * t:E * (t + 1)], ones_bf[:, :], chosen_sum[:, :], start=True, stop=False)
                        for u in range(t):
                            nc.tensor.matmul(bank[:, E * t:E * (t + 1)], ones_bf[:, :], chosen_bf[:, u, :], start=False, stop=False)
                        last = nc.tensor.matmul(bank[:, E * t:E * (t + 1)], tri_before[:, :], chosen_bf[:, t, :],
                                                start=False, stop=True)
                    last.then_inc(filled, 1)

            whole_program(pe, do)

        @block.scalar
        def _(act):
            act.sem_inc(exped, PRIME)
            act.sem_inc(o_copied, PRIME)
            for each in stacked.values():
                act.sem_inc(each, PRIME)
            act.sem_inc(x2_stored, PRIME)
            act.wait_ge(pool_ready, 3)
            act.wait_ge(cols_loaded, 16 * 4)

            def weights_high(i):
                act.wait_ge(w_loaded[i], 16)
                act.activation(w_hi[PART[i]][:, :, :], staging[i][:, :, :], ACT.Copy).then_inc(w_high, 1)

            for i in range(3):
                weights_high(i)

            def do(b, step):
                kind, a, n = step
                bank, free = bank_of(step), freed_by(step)
                if kind == "xT":
                    wait_filled(act, b, step)
                    if n >= 2:
                        act.wait_ge(xt_ready, b * (2 * NC_) + (n - 1))
                    for dst in (scaled[n % 2][:, :], xT_hi[:, n, :]):
                        last = act.activation(dst, bank[:, :], ACT.Identity, bias=bcol[:, n:n + 1], scale=gcol[:, n:n + 1])
                    last.then_inc(xt_hi, 1)
                    if first_batch(b) and n == NC_ - 1:
                        weights_high(3)
                elif kind in "qk":
                    buf, k = stack_use(a, n)
                    if a or n:
                        wait_stacked(act, b, kind, a * NC_ + n - 1)
                    wait_filled(act, b, step)
                    if a == 0:
                        bias = (bqcol if kind == "q" else bkcol)[:, n:n + 1]
                        act.activation(part[kind, "hi"][:, :], bank[:, :], ACT.Identity, bias=bias).then_inc(part_hi, 1)
                    else:
                        act.activation(part[kind, "hi"][:, :], bank[:, :], ACT.Copy).then_inc(part_hi, 1)
                elif kind == "scores":
                    g, qi, j = n // (NT * HG), n // HG % NT, n % HG
                    cols = P * (qi + 1)
                    act.wait_ge(maxed, b * (2 * HEADS) + (a * HEADS + n + 1))
                    if a == 1 and g >= 2 and qi == 0 and j == 0:
                        act.wait_ge(tail_ready, b * NC_ + (g - 1 + PRIME))
                    if a or n >= PROBS:
                        before = ("probsT", a, n - PROBS) if n >= PROBS else ("probsT", a - 1, HEADS + n - PROBS)
                        wait_filled(act, b, before)
                    act.activation(probs[n % PROBS][:, 0:cols], s_bank[n % 4][:, 0:cols], ACT.Exp,
                                   bias=neg_max[g % 2][:, qi, j:j + 1], scale=-1.0,
                                   accum_out=denom[g % 2][:, qi, j:j + 1]).then_inc(exped, 1)
                elif kind == "probsT" and n % 2 == 1:
                    wait_filled(act, b, step)
                    if a or n >= TURNED:
                        act.wait_ge(pv_done, b * (2 * UNITS) + (a * UNITS + (n - TURNED) // HG + 1))
                    cols = P * (n // HG % NT + 1)
                    act.activation(probsT[n % TURNED][:, 0:cols], bank[:, 0:cols], ACT.Copy).then_inc(free, 1)
                elif kind == "outcopy":
                    act.wait_ge(pv_done, b * (2 * UNITS) + (a * UNITS + NT * (n + 1)))
                    if a or n:
                        wait_filled(act, b, ("outT", a, n - 1) if n else ("outT", a - 1, NC_ - 1))
                    act.activation(outT[:, :], o_bank[:, :], ACT.Copy).then_inc(o_copied, 1)
                elif kind == "masked":
                    act.wait_ge(tail_ready, b * NC_ + (n + PRIME))
                    act.activation(e_mask[:, :, :], neg_max[n % 2][:, :, :], ACT.Exp, bias=minus_bias[:, 0:1]).then_inc(e_ready, 1)
                elif kind == "oT":
                    wait_filled(act, b, step)
                    act.activation(xT_hi[:, n, :], bank[:, :], ACT.Copy).then_inc(xt_hi, 1)
                elif kind == "suffix":
                    wait_filled(act, b, step)
                    act.activation(suffix[:, n, :], bank[:, :], ACT.Copy).then_inc(free, 1)
                elif kind == "x2T":
                    wait_filled(act, b, step)
                    act.activation(suffix[:, n, :], bank[:, :], ACT.Copy).then_inc(free, 1)
                elif kind == "logits":
                    act.wait_ge(logits_ready, b + 1)
                    for t in range(NT):
                        last = act.activation(gates[:, t, :], logit[:, t, :], ACT.Exp, bias=neg_top[:, t:t + 1])
                    last.then_inc(gexp_ready, 1)

            whole_program(act, do, copies_first(STEPS))

        @block.vector
        def _(dve):
            for r in range(RING):
                dve.sem_inc(freed[r], PRIME)
            dve.sem_inc(x_used, 1)
            dve.wait_ge(pool_ready, 3)
            def weights_low(i):
                dve.wait_ge(w_high, i + 1)
                dve.tensor_tensor(w_lo[PART[i]][:, :, :], staging[i][:, :, :], w_hi[PART[i]][:, :, :],
                                  ALU.subtract).then_inc(dve_ready, 1)

            def moments(i, src, t):
                dve.bn_stats(stats[i][:, t, :], src[:, t, :])

            def aggregate(i):
                dve.drain()
                for t in range(NT):
                    last = dve.bn_aggr(mv[i][:, t, :], stats[i][:, t, :])
                last.then_inc(stat_ready[i], 1)

            def normalize(i, count, src, dst):
                dve.wait_ge(rstd_ready[i], count)
                settle(dve)
                for t in range(NT):
                    last = dve.tensor_scalar(dst[:, t, :], src[:, t, :], mv[i][:, t, 0:1], rstd[i][:, t:t + 1],
                                             ALU.subtract, ALU.mult)
                last.then_inc(normed[i], 1)

            def do(b, step):
                kind, a, n = step
                bank, free = bank_of(step), freed_by(step)
                if kind == "moments0":
                    if n == 0:
                        dve.wait_ge(x_loaded, b * 16 + 16)
                    moments(0, xin, n)
                    if n == NT - 1:
                        aggregate(0)
                elif kind == "norm0":
                    if not first_batch(b):
                        dve.wait_ge(pv_done, b * (2 * UNITS))
                    normalize(0, b + 1, xin, ctxv)
                    if first_batch(b):
                        weights_low(0)
                        weights_low(1)
                elif kind == "xT":
                    dve.wait_ge(xt_hi, b * (2 * NC_) + (n + 1))
                    dve.tensor_tensor(xT_lo[:, n, :], scaled[n % 2][:, :], xT_hi[:, n, :], ALU.subtract).then_inc(xt_ready, 1)
                    if first_batch(b) and n == NC_ - 1:
                        weights_low(2)
                        weights_low(3)
                        dve.wait_ge(consts_loaded, 16 * 3)
                elif kind in "qk":
                    dve.wait_ge(part_hi, b * (4 * NC_) + (MADE[step] + 1))
                    if a == 0:
                        bias = (bqcol if kind == "q" else bkcol)[:, n:n + 1]
                        dve.scalar_tensor_tensor(out=part[kind, "lo"][:, :], in0=bank[:, :], scalar=bias,
                                                 in1=part[kind, "hi"][:, :], op0=ALU.add, op1=ALU.subtract).then_inc(free, 1)
                    else:
                        dve.tensor_tensor(part[kind, "lo"][:, :], bank[:, :], part[kind, "hi"][:, :], ALU.subtract).then_inc(free, 1)
                elif kind == "v":
                    wait_filled(dve, b, step)
                    dve.tensor_tensor(vals[:, n, :], bank[:, :], bv_rows[:, :], ALU.add).then_inc(free, 1)
                elif kind == "scores":
                    g, qi, j = n // (NT * HG), n // HG % NT, n % HG
                    cols = P * (qi + 1)
                    s = s_bank[n % 4][:, 0:cols]
                    first = BIG if a == 0 else least[:, qi // (NT - 1):qi // (NT - 1) + 1]
                    dve.wait_ge(scored, b * (2 * HEADS) + (a * HEADS + n + 1 + PRIME))
                    settle(dve)
                    dve.tensor_tensor_reduce(s, s, mask[:, S - cols:S], -SCALE, first, ALU.add, ALU.min,
                                             neg_max[g % 2][:, qi, j:j + 1]).then_inc(maxed, 1)
                elif kind == "probsT" and n % 2 == 0:
                    wait_filled(dve, b, step)
                    if a or n >= TURNED:
                        dve.wait_ge(pv_done, b * (2 * UNITS) + (a * UNITS + (n - TURNED) // HG + 1))
                    cols = P * (n // HG % NT + 1)
                    dve.tensor_copy(probsT[n % TURNED][:, 0:cols], bank[:, 0:cols]).then_inc(free, 1)
                elif kind == "normalize":
                    use = ring_use(("outT", a, n))
                    free = freed[use[1]]
                    o_back = ring[use[1]][:, :].rearrange("p (t n) -> p t n", n=P)
                    if a == 0:
                        if n == 0:
                            dve.wait_ge(x2_stored, b * 32 + PRIME)
                            settle(dve)
                        dve.wait_ge(exped, b * (2 * HEADS) + (NT * HG * (n + 1) + PRIME))
                        settle(dve)
                        dve.reciprocal(rdenom[:, :, :], denom[n % 2][:, :, :])
                        dve.drain()
                        wait_filled(dve, b, ("outT", a, n))
                        dve.tensor_tensor(o_sb[:, :, n * P:(n + 1) * P].rearrange("p t (j d) -> p t j d", d=DH),
                                          o_back.rearrange("p t (j d) -> p t j d", d=DH),
                                          rdenom[:, :, :].unsqueeze(3).to_broadcast([P, NT, HG, DH]), ALU.mult).then_inc(free, 1)
                        dve.drain().then_inc(o_normed, 1)
                    else:
                        dve.wait_ge(tail_ready, b * NC_ + (n + 1 + PRIME))
                        settle(dve)
                        dve.reciprocal(rdenom[:, :, :], e_cnt[:, :, :])
                        wait_filled(dve, b, ("outT", a, n))
                        dve.tensor_tensor(tail[:, :, :], o_back, tail[:, :, :], ALU.add).then_inc(free, 1)
                        dve.drain().then_inc(o_raw, 1)
                elif kind == "oT":
                    dve.wait_ge(xt_hi, b * (2 * NC_) + (NC_ + n + 1))
                    dve.tensor_tensor(xT_lo[:, n, :], bank[:, :], xT_hi[:, n, :], ALU.subtract).then_inc(free, 1)
                    dve.drain().then_inc(xt_ready, 1)
                elif kind == "proj":
                    if n == 0:
                        dve.wait_ge(res_ready, b + 1)
                        settle(dve)
                        dve.drain().then_inc(x_used, 1)
                    dve.wait_ge(projected, b * NT + (n + 1))
                    dve.tensor_tensor(x1[:, n, :], s_bank[n][:, :], x1[:, n, :], ALU.add)
                    dve.drain()
                    moments(1, x1, n)
                elif kind == "norm1":
                    aggregate(1)
                    normalize(1, b * 2 + 1, x1, x1)
                elif kind == "residual":
                    dve.wait_ge(resid_done, b * NC_ + NC_)
                    settle(dve)
                    for t in range(NT):
                        moments(1, o_sb, t)
                    aggregate(1)
                elif kind == "norm2":
                    normalize(1, b * 2 + 2, o_sb, o_sb)
                elif kind == "logits":
                    dve.wait_ge(slots_free, b + 1)
                    wait_filled(dve, b, step)
                    dve.tensor_copy(logit[:, :, :], bank[:, 0:NT * E].rearrange("p (t e) -> p t e", e=E)).then_inc(free, 1)
                    dve.drain()
                    for t in range(NT):
                        dve.max(top[:, t, :], logit[:, t, :])
                    dve.drain()
                    dve.tensor_scalar(neg_top[:, :], top[:, :, 0], -1.0, None, ALU.mult).then_inc(logits_ready, 1)
                    for t in range(NT):
                        dve.match_replace(left[:, t, :], top[:, t, :], logit[:, t, :], MASKED)
                    dve.drain()
                    dve.tensor_tensor(chosen[:, :, :], left[:, :, :], logit[:, :, :], ALU.not_equal)
                    dve.drain()
                    dve.tensor_copy(chosen_bf[:, :, :], chosen[:, :, :]).then_inc(chosen_ready, 1)
                    dve.wait_ge(gexp_ready, b + 1)
                    dve.tensor_tensor(gates[:, :, :], gates[:, :, :], chosen[:, :, :], ALU.mult)
                    dve.drain()
                    dve.tensor_reduce(gsum[:, :], gates[:, :, :], AX.X, ALU.add)
                    dve.drain()
                    dve.reciprocal(rgsum[:, :], gsum[:, :])
                    dve.drain()
                    for t in range(NT):
                        dve.tensor_scalar(gates[:, t, :], gates[:, t, :], rgsum[:, t:t + 1], None, ALU.mult)
                elif kind == "places":
                    wait_filled(dve, b, step)
                    count = bank[:, 0:NT * E].rearrange("p (t e) -> p t e", e=E)
                    dve.tensor_scalar(wrap[:, :, :], count, float(P), -(P * P - 1.0), ALU.is_ge, ALU.mult)
                    dve.scalar_tensor_tensor(out=place[:, :, :], in0=count, scalar=float(P), in1=col2e[:, :, :],
                                             op0=ALU.mult, op1=ALU.add)
                    dve.drain()
                    dve.tensor_tensor(place[:, :, :], place[:, :, :], wrap[:, :, :], ALU.add)
                    dve.scalar_tensor_tensor(out=chosen[:, :, :], in0=count, scalar=float(CAP), in1=chosen[:, :, :],
                                             op0=ALU.is_lt, op1=ALU.mult).then_inc(free, 1)
                    for t in range(NT):
                        dve.tensor_tensor(chosen_sum[:, :], chosen_sum[:, :], chosen_bf[:, t, :], ALU.add)
                        dve.drain()
                    dve.tensor_tensor(place[:, :, :], place[:, :, :], chosen[:, :, :], ALU.mult)
                    dve.drain()
                    for t in range(NT):
                        dve.max(key8[:, t, :], place[:, t, :])
                    dve.drain()
                    dve.tensor_scalar(gone8[:, :, :], key8[:, :, :], 0.0, 65536.0, ALU.is_equal, ALU.mult)
                    dve.drain()
                    dve.scalar_tensor_tensor(out=slot8[:, :, :], in0=key8[:, :, :], scalar=-1.0, in1=gone8[:, :, :],
                                             op0=ALU.add, op1=ALU.add).then_inc(routed, 1)

            whole_program(dve, do)


RT = CAP // P
MIX = I - P
GU = 2 * I
QUAD = 4


def expert_phase(nc, gate_up, down, xg, acc, table):
    with ExitStack() as ctx:
        def sb(name, shape, dt=F32):
            return ctx.enter_context(nc.sbuf_tensor(name, shape, dt))

        def sem(name):
            return ctx.enter_context(nc.semaphore(name))

        slots = sb("slots", [P, P + RT], I32)
        idx = [sb(f"idx{i}", [P, RT], I32) for i in range(4)]
        scatter_idx = [sb(f"scatter_idx{i}", [P, RT], I32) for i in range(2)]
        xe = [sb(f"xe{i}", [P, RT, XROW]) for i in range(4)]
        gate_col = [sb(f"gate_col{i}", [P, RT, 1]) for i in range(4)]
        gu = [sb(f"gu{i}", [P, NC_, GU]) for i in range(2)]
        gu_hi = [sb(f"gu_hi{i}", [P, NC_, GU], F32R) for i in range(2)]
        gu_lo = [sb(f"gu_lo{i}", [P, NC_, GU], F32R) for i in range(2)]
        dn = [sb(f"dn{i}", [P, 2, D]) for i in range(2)]
        dn_hi = [sb(f"dn_hi{i}", [P, 2, D], F32R) for i in range(2)]
        dn_lo = [sb(f"dn_lo{i}", [P, D], F32R) for i in range(2)]
        xT_hi = [sb(f"exT_hi{i}", [P, NC_, CAP], F32R) for i in range(2)]
        xT_lo = [sb(f"exT_lo{i}", [P, NC_, CAP], F32R) for i in range(2)]
        silu = [sb(f"silu{i}", [P, 2, CAP]) for i in range(2)]
        h = [sb(f"h{i}", [P, 2, CAP]) for i in range(2)]
        h_hi = [sb(f"h_hi{i}", [P, 2, CAP], F32R) for i in range(2)]
        h_lo = [sb(f"h_lo{i}", [P, 2, CAP], F32R) for i in range(2)]
        y = [sb(f"y{i}", [P, RT, D]) for i in range(2)]
        ident = sb("eident", [P, P])

        ps_x = ctx.enter_context(nc.psum_tensor("ps_x", [P, NC_, CAP], F32))
        ps_gu = [ctx.enter_context(nc.psum_tensor(f"ps_gu{i}", [P, 2, 512], F32)) for i in range(2)]
        ps_y = ctx.enter_context(nc.psum_tensor("ps_y", [P, RT, D], F32))

        e_const = sem("e_const")
        settled = sem("e_settled")
        slots_loaded = sem("slots_loaded")
        gu_loaded = [sem(f"gu_loaded{i}") for i in range(2)]
        dn_loaded = [sem(f"dn_loaded{i}") for i in range(2)]
        gathered = [sem(f"gathered{i}") for i in range(4)]
        scattered = sem("scattered")
        added = sem("added")
        idx_ready = sem("idx_ready")
        gates_copied = sem("gates_copied")
        scatter_idx_ready = sem("scatter_idx_ready")
        gu_hi_done = sem("gu_hi_done")
        gu_lo_done = sem("gu_lo_done")
        dn_hi_done = sem("dn_hi_done")
        dn_lo_done = sem("dn_lo_done")
        x_turned = sem("x_turned")
        x_hi_done = sem("x_hi_done")
        x_lo_done = sem("x_lo_done")
        gu_done = sem("gu_done")
        silu_done = sem("silu_done")
        h_done = sem("h_done")
        h_hi_done = sem("h_hi_done")
        h_lo_done = sem("h_lo_done")
        y_filled = sem("y_filled")
        y_read = sem("y_read")

        block = ctx.enter_context(nc.Block())

        def quads(eng, step):
            with eng.Fori(0, E // QUAD - 1) as q:
                for u in range(QUAD):
                    step(q, u, False)
            for u in range(QUAD):
                step(E // QUAD - 1, u, True)

        def count(q, u, ring=1):
            return q * (QUAD // ring) + (u // ring + 1)

        def settle(eng):
            eng.sem_inc(settled, 1)

        @block.sync
        def _(sp):
            sp.dma_start(slots[:, 0:P], table.rearrange("(p n) a -> p (n a)", p=P)).then_inc(slots_loaded, 16)
            sp.wait_ge(e_const, 2)
            with sp.Fori(0, E // QUAD) as q:
                for u in range(QUAD):
                    e = q * QUAD + u
                    i = u % 2
                    sp.wait_ge(gu_lo_done, count(q, u))
                    sp.dma_start(gu[i][:, :, :], gate_up[bass.ds(e, 1), :, :].rearrange("a (p c) n -> (a p) c n", c=NC_)).then_inc(gu_loaded[i], 16)
                    sp.wait_ge(dn_lo_done, count(q, u))
                    sp.dma_start(dn[i][:, 0, :], down[bass.ds(e, 1), 0:P, :].rearrange("a p n -> (a p) n")).then_inc(dn_loaded[i], 16)
                    sp.dma_start(dn[i][P - MIX:P, 1, :], down[bass.ds(e, 1), P:I, :].rearrange("a p n -> (a p) n")).then_inc(dn_loaded[i], 16)

        @block.gpsimd
        def _(pool):
            pool.memset(ident[:, :], 0.0).then_inc(e_const, 1)
            pool.iota(slots[:, P:P + RT], [[P, RT]], base=TOK, channel_multiplier=1)
            pool.wait_ge(e_const, 1)
            pool.affine_select(out=ident[:, :], in_=ident[:, :], compare_op=ALU.not_equal, fill=1.0,
                               base=0, pattern=[[-1, P]], channel_multiplier=1).then_inc(e_const, 1)

            def gather(q, u):
                i = u % 4
                e = q * QUAD + u
                settle(pool)
                pool.tensor_copy(idx[i][:, :], slots[:, bass.ds(e * RT, RT)]).then_inc(idx_ready, 1)
                pool.wait_ge(idx_ready, count(q, u))
                settle(pool)
                for t in range(RT):
                    pool.indirect_dma_start(xe[i][:, t, :], None, xg,
                                            bass.IndirectOffsetOnAxis(ap=idx[i][:, t:t + 1], axis=0)).then_inc(gathered[i], 16)

            def next_gather(q, u):
                pool.wait_ge(gates_copied, q * QUAD + (u + 2))
                gather(q, u + QUAD + 1)

            def step(q, u, last):
                pool.tensor_copy(scatter_idx[u % 2][:, :], slots[:, bass.ds((q * QUAD + u) * RT, RT)]).then_inc(scatter_idx_ready, 1)
                pool.wait_ge(scatter_idx_ready, count(q, u))
                pool.wait_ge(y_read, q * QUAD + (u + 3))
                settle(pool)
                for t in range(RT):
                    pool.indirect_dma_start(acc, bass.IndirectOffsetOnAxis(ap=scatter_idx[u % 2][:, t:t + 1], axis=0),
                                            y[u % 2][:, t, :], None, compute_op=ALU.add).then_inc(scattered, 16)
                if not last:
                    next_gather(q, u)
                pool.wait_ge(scattered, (q * QUAD + (u + 1)) * (16 * RT))
                pool.sem_inc(added, 1)

            pool.wait_ge(slots_loaded, 16)
            for u in range(QUAD):
                gather(0, u)
            next_gather(0, -1)
            quads(pool, step)
            pool.wait_ge(gathered[0], (E // QUAD + 1) * (16 * RT))

        @block.tensor
        def _(pe):
            def turn(q, u):
                pe.wait_ge(gathered[u % 4], (q + (u // 4 + 1)) * (16 * RT))
                pe.wait_ge(x_lo_done, q * QUAD + (u + 1))
                for t in range(RT):
                    for c in range(NC_):
                        last = nc.tensor.transpose(ps_x[:, c, t * P:(t + 1) * P], xe[u % 4][:, t, c:D:NC_], ident[:, :])
                last.then_inc(x_turned, 1)

            def three_passes(dst, pairs):
                ops = [(s, m) for s_hi, s_lo, m_hi, m_lo in pairs for s, m in ((s_hi, m_hi), (s_hi, m_lo), (s_lo, m_hi))]
                for n, (s, m) in enumerate(ops):
                    last = nc.tensor.matmul(dst, s, m, start=(n == 0), stop=(n == len(ops) - 1))
                return last

            def inner(q, u):
                i = u % 2
                pe.wait_ge(gu_lo_done, q * QUAD + (u + 1 + 2))
                pe.wait_ge(x_lo_done, q * QUAD + (u + 1 + 1))
                pe.wait_ge(h_done, q * QUAD + (u - 1 + 2))
                dsts = (ps_gu[i][:, 0, 0:CAP], ps_gu[i][:, 0, CAP:2 * CAP], ps_gu[i][:, 1, 0:CAP])
                for m, dst in enumerate(dsts):
                    cols = slice(m * P, (m + 1) * P)
                    last = three_passes(dst, [(gu_hi[i][:, c, cols], gu_lo[i][:, c, cols], xT_hi[i][:, c, :], xT_lo[i][:, c, :])
                                              for c in range(NC_)])
                last.then_inc(gu_done, 1)

            def outer(q, u):
                i = u % 2
                pe.wait_ge(dn_lo_done, q * QUAD + (u + 1 + 2))
                pe.wait_ge(h_lo_done, q * QUAD + (u + 1))
                pe.wait_ge(y_read, q * QUAD + (u + 2))
                for t in range(RT):
                    rows = slice(t * P, (t + 1) * P)
                    ops = ((h_hi[i][:, 0, rows], dn_hi[i][:, 0, :]), (h_hi[i][:, 0, rows], dn_lo[i][:, :]),
                           (h_lo[i][:, 0, rows], dn_hi[i][:, 0, :]), (h_hi[i][:, 1, rows], dn_hi[i][:, 1, :]),
                           (h_lo[i][:, 1, rows], dn_hi[i][:, 1, :]))
                    for n, (s, m) in enumerate(ops):
                        last = nc.tensor.matmul(ps_y[:, t, :], s, m, start=(n == 0), stop=(n == len(ops) - 1))
                last.then_inc(y_filled, 1)

            def step(q, u, last):
                if not (last and u + 2 >= QUAD):
                    turn(q, u + 2)
                if not (last and u + 1 >= QUAD):
                    inner(q, u + 1)
                outer(q, u)

            pe.sem_inc(gu_done, 2)
            pe.wait_ge(e_const, 2)
            turn(0, 0)
            turn(0, 1)
            inner(0, 0)
            quads(pe, step)

        @block.scalar
        def _(act):
            def high_gu(q, u):
                i = u % 2
                act.wait_ge(gu_loaded[i], (q * 2 + (u // 2 + 1)) * 16)
                act.wait_ge(gu_done, q * QUAD + (u - 1 + 2))
                act.activation(gu_hi[i][:, :, :], gu[i][:, :, :], ACT.Copy).then_inc(gu_hi_done, 1)

            def high_dn(q, u):
                i = u % 2
                act.wait_ge(dn_loaded[i], (q * 2 + (u // 2 + 1)) * 32)
                act.wait_ge(y_filled, q * QUAD + (u - 1 + 2))
                act.activation(dn_hi[i][P - MIX:P, 1, :], dn[i][P - MIX:P, 1, :], ACT.Copy)
                act.activation(dn_hi[i][:, 0, :], dn[i][:, 0, :], ACT.Copy).then_inc(dn_hi_done, 1)

            def high_x(q, u):
                act.wait_ge(x_turned, q * QUAD + (u + 1))
                act.wait_ge(gu_done, q * QUAD + (u - 1 + 2))
                act.activation(xT_hi[u % 2][:, :, :], ps_x[:, :, :], ACT.Copy).then_inc(x_hi_done, 1)

            def gate(q, u):
                i = u % 2
                act.wait_ge(gu_done, q * QUAD + (u + 1 + 2))
                act.wait_ge(h_done, q * QUAD + (u - 1 + 2))
                act.activation(silu[i][:, 0, :], ps_gu[i][:, 0, 0:CAP], ACT.Silu)
                act.activation(silu[i][P - MIX:P, 1, :], ps_gu[i][0:MIX, 1, 0:CAP], ACT.Silu).then_inc(silu_done, 1)

            def high_h(q, u):
                i = u % 2
                act.wait_ge(h_done, q * QUAD + (u + 1 + 2))
                act.wait_ge(y_filled, q * QUAD + (u - 1 + 2))
                act.activation(h_hi[i][:, :, :], h[i][:, :, :], ACT.Copy).then_inc(h_hi_done, 1)

            def weigh(q, u):
                i = u % 2
                act.wait_ge(y_filled, q * QUAD + (u + 1 + 2))
                act.wait_ge(gates_copied, q * QUAD + (u + 1))
                act.wait_ge(added, q * QUAD + (u - 1 + 2))
                settle(act)
                for t in range(RT):
                    last = act.activation(y[i][:, t, :], ps_y[:, t, :], ACT.Identity, scale=gate_col[u % 4][:, t, :])
                last.then_inc(y_read, 1)

            def step(q, u, last):
                if not (last and u + 2 >= QUAD):
                    high_x(q, u + 2)
                if not (last and u + 1 >= QUAD):
                    gate(q, u + 1)
                    high_dn(q, u + 1)
                    high_h(q, u + 1)
                weigh(q, u)
                if not (last and u + 3 >= QUAD):
                    high_gu(q, u + 3)

            act.sem_inc(y_filled, 2)
            act.sem_inc(added, 2)
            act.sem_inc(y_read, 2)
            act.wait_ge(e_const, 2)
            high_gu(0, 0)
            high_x(0, 0)
            high_dn(0, 0)
            high_gu(0, 1)
            high_x(0, 1)
            gate(0, 0)
            high_h(0, 0)
            high_gu(0, 2)
            quads(act, step)

        @block.vector
        def _(dve):
            def low_gu(q, u):
                i = u % 2
                dve.wait_ge(gu_hi_done, q * QUAD + (u + 1))
                dve.tensor_tensor(gu_lo[i][:, :, :], gu[i][:, :, :], gu_hi[i][:, :, :], ALU.subtract).then_inc(gu_lo_done, 1)

            def low_dn(q, u):
                i = u % 2
                dve.wait_ge(dn_hi_done, q * QUAD + (u + 1))
                dve.tensor_tensor(dn_hi[i][0:MIX, 1, :], dn[i][P - MIX:P, 1, :], dn_hi[i][P - MIX:P, 1, :], ALU.subtract)
                dve.tensor_tensor(dn_lo[i][:, :], dn[i][:, 0, :], dn_hi[i][:, 0, :], ALU.subtract).then_inc(dn_lo_done, 1)

            def low_x(q, u):
                dve.wait_ge(x_hi_done, q * QUAD + (u + 1))
                dve.tensor_tensor(xT_lo[u % 2][:, :, :], ps_x[:, :, :], xT_hi[u % 2][:, :, :], ALU.subtract).then_inc(x_lo_done, 1)
                e = q * QUAD + u
                dve.tensor_copy(gate_col[u % 4][:, :, :], xe[u % 4][:, :, bass.ds(D + e, 1)]).then_inc(gates_copied, 1)

            def product(q, u):
                i = u % 2
                dve.wait_ge(silu_done, q * QUAD + (u + 1))
                dve.tensor_tensor(h[i][:, 0, :], silu[i][:, 0, :], ps_gu[i][:, 0, CAP:2 * CAP], ALU.mult)
                for rows in (slice(0, MIX), slice(P - MIX, P)):
                    last = dve.tensor_tensor(h[i][rows, 1, :], silu[i][P - MIX:P, 1, :], ps_gu[i][P - MIX:P, 1, 0:CAP], ALU.mult)
                last.then_inc(h_done, 1)

            def low_h(q, u):
                i = u % 2
                dve.wait_ge(h_hi_done, q * QUAD + (u + 1))
                dve.tensor_tensor(h_lo[i][:, :, :], h[i][:, :, :], h_hi[i][:, :, :], ALU.subtract).then_inc(h_lo_done, 1)

            def step(q, u, last):
                if not (last and u + 2 >= QUAD):
                    low_x(q, u + 2)
                if not (last and u + 1 >= QUAD):
                    product(q, u + 1)
                    low_dn(q, u + 1)
                    low_h(q, u + 1)
                if not (last and u + 3 >= QUAD):
                    low_gu(q, u + 3)

            dve.sem_inc(gu_lo_done, 2)
            dve.sem_inc(dn_lo_done, 2)
            dve.sem_inc(h_done, 2)
            dve.sem_inc(x_lo_done, 1)
            low_gu(0, 0)
            low_x(0, 0)
            low_dn(0, 0)
            low_gu(0, 1)
            low_x(0, 1)
            product(0, 0)
            low_h(0, 0)
            low_gu(0, 2)
            quads(dve, step)


def final_phase(nc, acc, out):
    with ExitStack() as ctx:
        def sb(name, shape, dt=F32):
            return ctx.enter_context(nc.sbuf_tensor(name, shape, dt))

        def sem(name):
            return ctx.enter_context(nc.semaphore(name))

        r = [sb(f"r{b}", [P, NT, D]) for b in range(B)]
        stats = sb("fstats", [P, B, NT, 6])
        mv = sb("fmv", [P, B, NT, 2])
        var = sb("fvar", [P, B, NT])
        rstd = sb("frstd", [P, B, NT])
        power = sb("fpower", [P, NT])
        loaded = [sem(f"loaded{b}") for b in range(B)]
        f_const = sem("f_const")
        f_moments = sem("f_moments")
        f_var = sem("f_var")
        f_rstd = sem("f_rstd")
        f_normed = sem("f_normed")
        stored = sem("stored")
        block = ctx.enter_context(nc.Block())

        @block.sync
        def _(sp):
            for b in range(B):
                sp.dma_start(r[b][:, :, :], acc[b * S:(b + 1) * S, :].rearrange("(t p) d -> p t d", p=P)).then_inc(loaded[b], 16)
            for b in range(B):
                sp.wait_ge(f_normed, b + 1)
                sp.dma_start(out[b].rearrange("(t p) d -> p t d", p=P), r[b][:, :, :]).then_inc(stored, 16)
            sp.wait_ge(stored, 16 * B)

        @block.gpsimd
        def _(pool):
            pool.memset(power[:, :], -0.5).then_inc(f_const, 1)
            for b in range(B):
                pool.wait_ge(f_moments, b + 1)
                pool.tensor_scalar(var[:, b, :], mv[:, b, :, 1], EPS, 0.0, ALU.add, ALU.add).then_inc(f_var, 1)
                pool.wait_ge(f_const, 1)
                pool.wait_ge(f_var, b + 1)
                pool.tensor_tensor(rstd[:, b, :], var[:, b, :], power[:, :], ALU.pow).then_inc(f_rstd, 1)

        @block.vector
        def _(dve):
            def moments(b):
                dve.wait_ge(loaded[b], 16)
                for t in range(NT):
                    dve.bn_stats(stats[:, b, t, :], r[b][:, t, :])
                dve.drain()
                for t in range(NT):
                    last = dve.bn_aggr(mv[:, b, t, :], stats[:, b, t, :])
                last.then_inc(f_moments, 1)

            moments(0)
            for b in range(B):
                if b + 1 < B:
                    moments(b + 1)
                dve.wait_ge(f_rstd, b + 1)
                for t in range(NT):
                    last = dve.tensor_scalar(r[b][:, t, :], r[b][:, t, :], mv[:, b, t, 0:1], rstd[:, b, t:t + 1],
                                             ALU.subtract, ALU.mult)
                last.then_inc(f_normed, 1)


_INS = ['x', 'ctx_2048', 'L0_attn_ln_g', 'L0_attn_ln_b', 'L0_attn_Wq', 'L0_attn_bq', 'L0_attn_Wk', 'L0_attn_bk',
        'L0_attn_Wv', 'L0_attn_bv', 'L0_attn_Wo', 'L0_attn_bo', 'L0_ffn_router_weight']


def kernel(**inputs):
    import numpy as _np
    import concourse.bacc as _bacc
    from concourse import mybir as _mybir
    from concourse.bass_utils import run_bass_kernel_spmd as _run

    given = {n: _np.ascontiguousarray(inputs[n]) for n in _INS}
    gate, up = _np.asarray(inputs['L0_ffn_gate_proj']), _np.asarray(inputs['L0_ffn_up_proj'])
    given['gate_up'] = _np.concatenate([gate[:, :, :P], up[:, :, :P], gate[:, :, P:], up[:, :, P:]], axis=2)
    given['down'] = _np.ascontiguousarray(inputs['L0_ffn_down_proj'])

    nc = _bacc.Bacc("TRN2", target_bir_lowering=False, num_devices=1)
    arrays, args = {}, []
    for name, a in given.items():
        arrays[f"in_{name}"] = a
        args.append(nc.dram_tensor(f"in_{name}", a.shape, _mybir.dt.from_np(a.dtype), kind="ExternalInput").ap())
    args.append(nc.dram_tensor("out_x", (B, S, D), F32, kind="ExternalOutput").ap())
    kernel_body(nc, *args)
    r = _run(nc, [arrays], core_ids=[0])
    return r.results[0]["out_x"]
```
